# Optimizing a Trainium2 kernel written in Bass

```python
import numpy as np
import jax
import jax.numpy as jnp

def _softmax(x, axis=-1):
    return jax.nn.softmax(x, axis=axis)

def _gelu(x):
    return jax.nn.gelu(x, approximate=True)

def _silu(x):
    return jax.nn.silu(x)

def _sigmoid(x):
    return jax.nn.sigmoid(x)

def _layernorm(x, axis=-1, eps=1e-05):
    m = jnp.mean(x, axis=axis, keepdims=True)
    v = jnp.var(x, axis=axis, keepdims=True)
    return (x - m) / jnp.sqrt(v + eps)

def _scatter_add(tgt, idx, src, axis=0):
    return tgt.at[idx].add(src)

def _segment_sum(src, seg, n):
    return jax.ops.segment_sum(src, seg, n)
kernel_name = 'mk_lm_tower_d1_tok_ids256_r4_c110ae'

def setup_inputs(seed: int=0):
    np.random.seed(seed)
    _w = jnp.asarray

    def _rec_inputs():
        import jax
        import jax.numpy as jnp
        _rk = jax.random.key(seed)
        x = jax.random.randint(jax.random.fold_in(_rk, 1), (64, 128), 0, 100, jnp.int32)
        mask_BSS_b0_1 = jnp.logical_not(jnp.ones((64, 128, 128), dtype=bool))
        fside_BSS_rel_dist = jax.random.uniform(jax.random.fold_in(_rk, 22), (64, 128, 128), jnp.float32, 0.0, 1)
        return (x, mask_BSS_b0_1, fside_BSS_rel_dist)
    x, mask_BSS_b0_1, fside_BSS_rel_dist = _rec_inputs()

    def _L0_tok_setup():
        import jax, jax.numpy as jnp
        import numpy as np
        NUM_ATOMS = 100
        DIM = 64
        LN_EPS = 1e-05
        key = jax.random.key(seed)
        ks = jax.random.split(key, 10)
        b, n, d = (4, 512, DIM)
        atom_ids = jax.random.randint(ks[0], (b, n), 0, NUM_ATOMS)
        adj_mat = jax.random.randint(ks[1], (b, n, n), 0, 2).astype(bool)
        rel_dist = jax.random.uniform(ks[2], (b, n, n), dtype=jnp.float32)
        s = 1.0 / np.sqrt(d)
        params = {'atom_embed': jax.random.normal(ks[3], (NUM_ATOMS, d), jnp.float32), 'neighbor_embed': jax.random.normal(ks[4], (NUM_ATOMS, d), jnp.float32), 'w_rd': jax.random.normal(ks[5], (d,), jnp.float32), 'w1': jax.random.normal(ks[6], (2 * d, d), jnp.float32) * s, 'b1': jnp.zeros((d,), jnp.float32), 'gamma': jnp.ones((d,), jnp.float32), 'beta': jnp.zeros((d,), jnp.float32), 'w2': jax.random.normal(ks[7], (d, d), jnp.float32) * s, 'b2': jnp.zeros((d,), jnp.float32)}
        return {'atom_ids': atom_ids, 'adj_mat': adj_mat, 'rel_dist': rel_dist, **params}
    _L0_tok_all = _L0_tok_setup()
    _L0_tok_in = {k: v for k, v in _L0_tok_all.items() if k in ('atom_embed', 'neighbor_embed', 'w_rd', 'w1', 'b1', 'gamma', 'beta', 'w2', 'b2')}
    del _L0_tok_all

    def _L0_attn_setup():
        import jax, jax.numpy as jnp
        import numpy as np
        N_HEADS, D_MODEL, D_HEAD = (8, 64, 32)
        BATCH, SEQ = (2, 512)
        INIT_RANGE = 0.02

        def _odd_causal_mask(S):
            i = jnp.arange(S)[:, None]
            j = jnp.arange(S)[None, :]
            allowed = (j < i) & (j % 2 == 1) | (i == j)
            return allowed
        key = jax.random.key(seed)
        ks = jax.random.split(key, 6)
        x = jax.random.normal(ks[0], (BATCH, SEQ, D_MODEL), dtype=jnp.float32)
        W_Q = INIT_RANGE * jax.random.normal(ks[1], (N_HEADS, D_MODEL, D_HEAD), dtype=jnp.float32)
        W_K = INIT_RANGE * jax.random.normal(ks[2], (N_HEADS, D_MODEL, D_HEAD), dtype=jnp.float32)
        W_V = INIT_RANGE * jax.random.normal(ks[3], (N_HEADS, D_MODEL, D_HEAD), dtype=jnp.float32)
        W_O = INIT_RANGE * jax.random.normal(ks[4], (N_HEADS, D_HEAD, D_MODEL), dtype=jnp.float32)
        b_Q = jnp.zeros((N_HEADS, D_HEAD), dtype=jnp.float32)
        b_K = jnp.zeros((N_HEADS, D_HEAD), dtype=jnp.float32)
        b_V = jnp.zeros((N_HEADS, D_HEAD), dtype=jnp.float32)
        b_O = jnp.zeros((D_MODEL,), dtype=jnp.float32)
        return {'normalized_resid_pre': x, 'W_Q': W_Q, 'W_K': W_K, 'W_V': W_V, 'W_O': W_O, 'b_Q': b_Q, 'b_K': b_K, 'b_V': b_V, 'b_O': b_O}
    _L0_attn_all = _L0_attn_setup()
    _L0_attn_in = {k: v for k, v in _L0_attn_all.items() if k in ('W_Q', 'W_K', 'W_V', 'W_O', 'b_Q', 'b_K', 'b_V', 'b_O')}
    del _L0_attn_all

    def _L0_ffn_setup():
        import jax, jax.numpy as jnp
        import numpy as np
        D_MODEL = 64
        N_EXPERTS = 16
        HIDDEN = 128
        SCALE = 0.02
        key = jax.random.key(seed)
        ks = jax.random.split(key, 5)
        x = jax.random.normal(ks[0], (4, 2048, D_MODEL), dtype=jnp.float32)
        gate_w = jax.random.normal(ks[1], (D_MODEL, N_EXPERTS), dtype=jnp.float32) * SCALE
        gate_b = jnp.zeros((N_EXPERTS,), dtype=jnp.float32)
        w1 = jax.random.normal(ks[2], (N_EXPERTS, D_MODEL, HIDDEN), dtype=jnp.float32) * SCALE
        w2 = jax.random.normal(ks[3], (N_EXPERTS, D_MODEL, HIDDEN), dtype=jnp.float32) * SCALE
        w3 = jax.random.normal(ks[4], (N_EXPERTS, HIDDEN, D_MODEL), dtype=jnp.float32) * SCALE
        return {'x': x, 'gate_w': gate_w, 'gate_b': gate_b, 'w1': w1, 'w2': w2, 'w3': w3}
    _L0_ffn_all = _L0_ffn_setup()
    _L0_ffn_in = {k: v for k, v in _L0_ffn_all.items() if k in ('gate_w', 'gate_b', 'w1', 'w2', 'w3')}
    del _L0_ffn_all
    return {'x': x, 'mask_BSS_b0_1': mask_BSS_b0_1, 'fside_BSS_rel_dist': fside_BSS_rel_dist, 'L0_tok_atom_embed': _L0_tok_in['atom_embed'], 'L0_tok_neighbor_embed': _L0_tok_in['neighbor_embed'], 'L0_tok_w_rd': _L0_tok_in['w_rd'], 'L0_tok_w1': _L0_tok_in['w1'], 'L0_tok_b1': _L0_tok_in['b1'], 'L0_tok_gamma': _L0_tok_in['gamma'], 'L0_tok_beta': _L0_tok_in['beta'], 'L0_tok_w2': _L0_tok_in['w2'], 'L0_tok_b2': _L0_tok_in['b2'], 'L0_attn_W_Q': _L0_attn_in['W_Q'], 'L0_attn_W_K': _L0_attn_in['W_K'], 'L0_attn_W_V': _L0_attn_in['W_V'], 'L0_attn_W_O': _L0_attn_in['W_O'], 'L0_attn_b_Q': _L0_attn_in['b_Q'], 'L0_attn_b_K': _L0_attn_in['b_K'], 'L0_attn_b_V': _L0_attn_in['b_V'], 'L0_attn_b_O': _L0_attn_in['b_O'], 'L0_ffn_gate_w': _L0_ffn_in['gate_w'], 'L0_ffn_gate_b': _L0_ffn_in['gate_b'], 'L0_ffn_w1': _L0_ffn_in['w1'], 'L0_ffn_w2': _L0_ffn_in['w2'], 'L0_ffn_w3': _L0_ffn_in['w3']}

def reference(x, mask_BSS_b0_1, fside_BSS_rel_dist, L0_tok_atom_embed, L0_tok_neighbor_embed, L0_tok_w_rd, L0_tok_w1, L0_tok_b1, L0_tok_gamma, L0_tok_beta, L0_tok_w2, L0_tok_b2, L0_attn_W_Q, L0_attn_W_K, L0_attn_W_V, L0_attn_W_O, L0_attn_b_Q, L0_attn_b_K, L0_attn_b_V, L0_attn_b_O, L0_ffn_gate_w, L0_ffn_gate_b, L0_ffn_w1, L0_ffn_w2, L0_ffn_w3):
    import jax
    import jax.numpy as jnp

    def _L0_tok_ref(atom_ids, adj_mat, rel_dist, atom_embed, neighbor_embed, w_rd, w1, b1, gamma, beta, w2, b2):
        import jax, jax.numpy as jnp
        import numpy as np
        NUM_ATOMS = 100
        DIM = 64
        LN_EPS = 1e-05
        n = atom_ids.shape[-1]
        eye = jnp.eye(n, dtype=bool)
        mask = adj_mat & ~eye
        embeds = atom_embed[atom_ids]
        nbr_embeds = neighbor_embed[atom_ids]
        weighted = jnp.where(mask, rel_dist, jnp.zeros((), rel_dist.dtype))
        neighbor_feats = jnp.einsum('bij,bjd->bid', weighted, nbr_embeds) * w_rd
        x = jnp.concatenate([embeds, neighbor_feats], axis=-1)
        h = x @ w1 + b1
        mu = jnp.mean(h, axis=-1, keepdims=True)
        var = jnp.mean(jnp.square(h - mu), axis=-1, keepdims=True)
        h = (h - mu) * jax.lax.rsqrt(var + LN_EPS) * gamma + beta
        h = jax.nn.silu(h)
        return h @ w2 + b2

    def _L0_attn_ref(normalized_resid_pre, W_Q, W_K, W_V, W_O, b_Q, b_K, b_V, b_O):
        import jax, jax.numpy as jnp
        import numpy as np
        N_HEADS, D_MODEL, D_HEAD = (8, 64, 32)
        BATCH, SEQ = (2, 512)
        INIT_RANGE = 0.02

        def _odd_causal_mask(S):
            i = jnp.arange(S)[:, None]
            j = jnp.arange(S)[None, :]
            allowed = (j < i) & (j % 2 == 1) | (i == j)
            return allowed
        x = normalized_resid_pre
        q = jnp.einsum('bsm,hmd->bshd', x, W_Q) + b_Q
        k = jnp.einsum('bsm,hmd->bshd', x, W_K) + b_K
        v = jnp.einsum('bsm,hmd->bshd', x, W_V) + b_V
        scale = 1.0 / jnp.sqrt(jnp.float32(D_HEAD))
        scores = jnp.einsum('bqhd,bkhd->bhqk', q, k) * scale
        allowed = _odd_causal_mask(scores.shape[-1])
        scores = jnp.where(allowed, scores, -jnp.inf)
        pattern = jax.nn.softmax(scores, axis=-1)
        z = jnp.einsum('bkhd,bhqk->bqhd', v, pattern)
        return jnp.einsum('bqhd,hdm->bqm', z, W_O) + b_O

    def _L0_ffn_ref(x, gate_w, gate_b, w1, w2, w3):
        import jax, jax.numpy as jnp
        import numpy as np
        D_MODEL = 64
        N_EXPERTS = 16
        HIDDEN = 128
        SCALE = 0.02
        n_experts = w1.shape[0]
        logits = jnp.einsum('bsd,de->bse', x, gate_w) + gate_b
        probs = jax.nn.softmax(logits, axis=-1)
        top_probs, top_idx = jax.lax.top_k(probs, 2)
        top_probs = top_probs / jnp.sum(top_probs, axis=-1, keepdims=True)
        dispatch = jnp.sum(jax.nn.one_hot(top_idx, n_experts, dtype=x.dtype) * top_probs[..., None], axis=-2)
        h1 = jnp.einsum('bsd,edh->bseh', x, w1)
        h2 = jnp.einsum('bsd,edh->bseh', x, w2)
        hidden = jax.nn.silu(h1) * h2
        expert_out = jnp.einsum('bseh,eho->bseo', hidden, w3)
        return jnp.einsum('bseo,bse->bso', expert_out, dispatch)
    h = _L0_tok_ref(x, mask_BSS_b0_1, fside_BSS_rel_dist, L0_tok_atom_embed, L0_tok_neighbor_embed, L0_tok_w_rd, L0_tok_w1, L0_tok_b1, L0_tok_gamma, L0_tok_beta, L0_tok_w2, L0_tok_b2)
    h = h + _L0_attn_ref(_layernorm(h, axis=-1), L0_attn_W_Q, L0_attn_W_K, L0_attn_W_V, L0_attn_W_O, L0_attn_b_Q, L0_attn_b_K, L0_attn_b_V, L0_attn_b_O)
    h = h + _L0_ffn_ref(_layernorm(h, axis=-1), L0_ffn_gate_w, L0_ffn_gate_b, L0_ffn_w1, L0_ffn_w2, L0_ffn_w3)
    return h

_drawn_inputs = setup_inputs


def setup_inputs(seed=0):
    import zlib

    import numpy as np

    out = dict(_drawn_inputs(seed))
    spreads = {'L0_tok_b1': (0.0, 0.1),
     'L0_tok_gamma': (1.0, 0.2),
     'L0_tok_beta': (0.0, 0.1),
     'L0_tok_b2': (0.0, 0.1),
     'L0_attn_b_Q': (0.0, 0.8),
     'L0_attn_b_K': (0.0, 0.8),
     'L0_attn_b_V': (0.0, 0.1),
     'L0_attn_b_O': (0.0, 0.1),
     'L0_ffn_gate_b': (0.0, 0.8)}
    factors = {'L0_attn_W_Q': 8.0,
     'L0_attn_W_K': 8.0,
     'L0_ffn_gate_w': 8.0,
     'L0_ffn_w1': 8.0,
     'L0_ffn_w2': 8.0,
     'L0_ffn_w3': 8.0}
    for name, (base, spread) in spreads.items():
        noise = np.random.default_rng([zlib.crc32(name.encode()), seed]).standard_normal(out[name].shape)
        drawn = base * np.exp(spread * noise) if base else spread * noise
        out[name] = jnp.asarray(drawn.astype(out[name].dtype))
    for name, factor in factors.items():
        out[name] = (out[name] * factor).astype(out[name].dtype)
    return out
```

```python
from contextlib import ExitStack

import concourse.bass as bass
from concourse import mybir

ALU = mybir.AluOpType
ACT = mybir.ActivationFunctionType
AXX = mybir.AxisListType.X
F32 = mybir.dt.float32
BF16 = mybir.dt.bfloat16
I32 = mybir.dt.int32
U32 = mybir.dt.uint32
U8 = mybir.dt.uint8

P = 128
HALF = P // 2
GB = 4
NP = 2
BIG = 1.0e30
EPS = 1e-5


def lm_tower_kernel(
    nc, ids, adj, rel, atom_embed, neighbor_embed, w_rd, w1, b1, gamma, beta, w2, b2,
    W_Q, W_K, W_V, W_O, b_Q, b_K, b_V, b_O, gate_w, gate_b, ew1, ew2, ew3,
    out, sorted_rows, expert_out,
):
    NB, S = ids.shape
    D = w2.shape[0]
    H, _, DH = W_Q.shape
    NA = atom_embed.shape[0]
    NE, _, HID = ew1.shape
    NG = NB // GB
    NTOK = NB * S
    REG = NTOK + P
    TOPK = 2
    NT = TOPK * NTOK // P + NE
    ROW = D + 2
    DUMP = TOPK * NTOK
    NQ = NT // 4
    QB = 4
    SCALE = float(DH) ** -0.5
    assert S == P and D == HALF and H * DH == 2 * P and NG * GB == NB and NQ % QB == 0 and NE == 16

    with ExitStack() as ctx:
        def sb(name, shape, dt=F32):
            return ctx.enter_context(nc.sbuf_tensor(name, shape, dt))

        def sem(name):
            return ctx.enter_context(nc.semaphore(name))

        psum = [ctx.enter_context(nc.psum_tensor(f"bank{i}", [P, 512], F32)) for i in range(4)]
        ps_scores = ctx.enter_context(nc.psum_tensor("ps_scores", [P, 2, 512], F32))
        ps_z = ctx.enter_context(nc.psum_tensor("ps_z", [P, 2, 512], F32))
        ps_tok, ps_pt, ps_g0, ps_g1 = psum
        ps_g = [ps_g0, ps_g1]

        ident = sb("ident", [P, P])
        ident_b = sb("ident_b", [P, P], BF16)
        off_diag = sb("off_diag", [P, P])
        causal = sb("causal", [P, 512], BF16)
        before = sb("before", [P, P], BF16)
        ones_b = sb("ones_b", [P, P], BF16)
        head_sum = sb("head_sum", [P, 4])
        atom_no = sb("atom_no", [P, 1])
        rev_e = sb("rev_e", [P, NE])
        base_e = sb("base_e", [P, NE])
        dest = sb("dest", [P, 2, GB], I32)
        tmp_i = sb("tmp_i", [P, 64], I32)
        both_embed = sb("both_embed", [NA, 2 * D])
        embed_t = sb("embed_t", [P, NA])
        wrd_col = sb("wrd_col", [P, 1])
        w1_bd = sb("w1_bd", [P, 2 * D])
        b1_bc = sb("b1_bc", [NA, D])
        table = sb("table", [NA, 2 * D])
        table_r = sb("table_r", [NA, 2 * D])
        table_b = sb("table_b", [NA, 3, 2 * D], BF16)
        eps_col = sb("eps_col", [P, 1])
        film = sb("film", [P, 4])
        w2_bd = sb("w2_bd", [P, 2 * D])
        b2_bc = sb("b2_bc", [P, D])
        qkv_raw = sb("qkv_raw", [D, 3, H * DH])
        bias_col = sb("bias_col", [P, 3, 2])
        qkv_t = sb("qkv_t", [P, 3, 2, 2, D])
        qkv_w = sb("qkv_w", [P, 3, 2 * P])
        a_bd = sb("a_bd", [P, H, P])
        wo_sb = sb("wo_sb", [P, 2, D])
        bo_bc = sb("bo_bc", [P, D])
        gate_bd = sb("gate_bd", [P, 2 * NE])
        gateb_bc = sb("gateb_bc", [P, NE])
        ew12 = sb("ew12", [D, NE * 2 * HID])
        ew3_sb = sb("ew3_sb", [HID, NE * D])
        rel_sb = sb("rel_sb", [P, GB, P])
        adj_sb = sb("adj_sb", [P, GB, P], U8)
        adj_f = sb("adj_f", [P, GB, P])
        ids_sb = sb("ids_sb", [NA, GB, P], I32)
        weighted = sb("weighted", [P, GB, P])
        one_hot = sb("one_hot", [NA, GB, P], BF16)
        weighted_t = sb("weighted_t", [P, GB, P])
        nbr = sb("nbr", [P, GB, D])
        st_a = sb("st_a", [P, GB, 6])
        mv_a = sb("mv_a", [P, GB, 2])
        rs_a = sb("rs_a", [P, 2, GB])
        z_tok = sb("z_tok", [P, GB, D])
        en = sb("en", [P, 2, P])
        en1 = sb("en1", [P, 2, P])
        gz = sb("gz", [P, 2, P])
        hs = sb("hs", [P, 2, P])
        h_tok = sb("h_tok", [P, GB, D])
        st_b = sb("st_b", [P, GB, 6])
        mv_b = sb("mv_b", [P, GB, 2])
        rs_b = sb("rs_b", [P, 2, GB])
        y_tok = sb("y_tok", [P, GB, D])
        y_t = sb("y_t", [P, NP, P + HALF])
        g_sb = sb("g_sb", [P, H, NP, HALF])
        k_even = sb("k_even", [P, 2, 2, NP * HALF])
        qk_prod = sb("qk_prod", [P, 2, 2, NP * HALF])
        diag_s = sb("diag_s", [HALF, GB, H])
        v_odd = sb("v_odd", [P, GB, H // 2, 2, DH + 1])
        v_even = sb("v_even", [HALF, GB, H, DH])
        row_max = sb("row_max", [P, NP, 2 * H])
        probs = sb("probs", [P, NP, 2, H * HALF])
        p_diag = sb("p_diag", [HALF, NP, 2 * H])
        probs_t = sb("probs_t", [P, 2, 4, P])
        den = sb("den", [P, 2 * H])
        rden = sb("rden", [P, 2 * H])
        pdn = sb("pdn", [HALF, 2 * H])
        pv_even = sb("pv_even", [HALF, 2 * H, DH])
        zn = sb("zn", [P, 2 * H, DH])
        zt = sb("zt", [P, 2, 2, P])
        resid = sb("resid", [P, NB, D])
        st_c = sb("st_c", [P, GB, 6])
        mv_c = sb("mv_c", [P, GB, 2])
        rs_c = sb("rs_c", [P, 2, GB])
        rows = sb("rows", [P, 2, GB, ROW])
        y2 = sb("y2", [P, GB, D])
        y2_t = sb("y2_t", [P, 2, P])
        lg = sb("lg", [P, GB, NE])
        lg2 = sb("lg2", [P, GB, NE])
        mx = sb("mx", [P, 2, GB])
        eq = sb("eq", [P, 2, GB, NE])
        rk = sb("rk", [P, 2, GB])
        oh = sb("oh", [P, 2, GB, NE])
        picked = sb("picked", [P, GB, NE], BF16)
        picked_before = sb("picked_before", [P, GB, NE], BF16)
        picked_all = sb("picked_all", [P, NE], BF16)
        slot = sb("slot", [P, GB, NE])
        slot2 = sb("slot2", [P, 2, GB, NE])
        slot_f = sb("slot_f", [P, 2, GB])
        slot_u = sb("slot_u", [P, 2, GB], U32)
        dmx = sb("dmx", [P, GB])
        ex = sb("ex", [P, GB])
        ex1 = sb("ex1", [P, GB])
        wt = sb("wt", [P, 2, GB])

        pads = sb("pads", [P, 2 * NE, ROW])
        tile_no = sb("tile_no", [P, 2])
        count = sb("count", [P, NE])
        tail_row = sb("tail_row", [P, NE], I32)
        cnt_r = sb("cnt_r", [P, NE], I32)
        cnt_m = sb("cnt_m", [P, NE], I32)
        n_tiles = sb("n_tiles", [P, NE])
        ones_e = sb("ones_e", [P, NE])
        tiles_to = sb("tiles_to", [P, NE])
        past = sb("past", [P, 2, NE])
        past_n = sb("past_n", [P, 2, NE])
        tile_e = sb("tile_e", [P, 2])
        tile_s = sb("tile_s", [P, 2])
        tile_d = sb("tile_d", [P, 2])
        tile_vals = sb("tile_vals", [P, 4])
        tile_table = sb("tile_table", [1, 4 * P], I32)
        x_rows = sb("x_rows", [P, QB, 4, ROW])
        x_t = sb("x_t", [D, 2, 4, P])
        silu = sb("silu", [P, 2, 4, P])
        hidden = sb("hidden", [P, 2, 4, P])
        hidden_t = sb("hidden_t", [P, 2, 4, P])
        y_rows = sb("y_rows", [P, QB, 4, D])
        NCH = 4
        CB = NB // NCH
        picked_out = sb("picked_out", [P, 2, NB, D])

        tail_ready, pads_written, table_ready, out_ready, stored, cnt_psum, table_psum, dve_route, added = (
            sem(n) for n in ("tail_ready", "pads_written", "table_ready", "out_ready", "stored", "cnt_psum",
                             "table_psum", "dve_route", "added"))
        y_loaded = [sem(f"y_loaded{c}") for c in range(NCH)]
        x_loaded, rows_out = ([sem(f"{n}_q{q}") for q in range(QB)] for n in ("x_loaded", "rows_out"))
        xt_psum, xt_ready, up_psum, silu_ready, hid_ready, ht_psum, ht_ready, down_psum, o_ready = (
            [sem(f"{n}_{q}") for q in range(2)] for n in (
                "xt_psum", "xt_ready", "up_psum", "silu_ready", "hid_ready", "ht_psum", "ht_ready", "down_psum",
                "o_ready"))
        consts_loaded, waits_passed = sem("consts_loaded"), sem("waits_passed")
        pool_const, dve_const, act_const, pe_const = (sem(n) for n in (
            "pool_const", "dve_const", "act_const", "pe_const"))
        pair_loaded, ids_loaded, adj_ready = sem("pair_loaded"), sem("ids_loaded"), sem("adj_ready")
        masked, onehot_ready, transposed_w, wt_ready, nb_psum, nb_ready, tok_psum = (sem(n) for n in (
            "masked", "onehot_ready", "transposed_w", "wt_ready", "nb_psum", "nb_ready", "tok_psum"))
        a_stats, a_rstd, b_stats, b_rstd, c_stats, c_rstd = (
            sem(n) for n in ("a_stats", "a_rstd", "b_stats", "b_rstd", "c_stats", "c_rstd"))
        a_norm, z_ready, z_psum, exp_ready, gz_ready, hs_ready, w2_psum, h_ready = (
            sem(n) for n in ("a_norm", "z_ready", "z_psum", "exp_ready", "gz_ready", "hs_ready", "w2_psum", "h_ready"))
        b_norm, y_ready, y_psum, yt_ready, resid_set = (sem(n) for n in (
            "b_norm", "y_ready", "y_psum", "yt_ready", "resid_set"))
        g_psum = [sem(f"g_psum{i}") for i in range(2)]
        g_ready = [sem(f"g_ready{i}") for i in range(2)]
        qk_psum = [sem(f"qk_psum{i}") for i in range(2)]
        ke_ready = [sem(f"ke_ready{i}") for i in range(2)]
        prod_ready = [sem(f"prod_ready{i}") for i in range(2)]
        diag_psum, diag_ready = sem("diag_psum"), sem("diag_ready")
        v_psum = [sem(f"v_psum{b}") for b in range(GB)]
        v_ready = [sem(f"v_ready{b}") for b in range(GB)]
        s_psum, max_step, sub_ready, dsub_ready, p_ready, pd_ready = (
            [sem(f"{n}{p}") for p in range(NP)] for n in (
                "s_psum", "max_step", "sub_ready", "dsub_ready", "p_ready", "pd_ready"))
        pt_psum = [sem(f"pt_psum{b}") for b in range(GB)]
        pt_ready = [sem(f"pt_ready{b}") for b in range(GB)]
        z_done = [sem(f"z_done{b}") for b in range(GB)]
        z_step, zn_ready, zt_psum, zt_ready, wo_psum, h2_ready = (
            [sem(f"{n}_{p}") for p in range(NP)] for n in (
                "z_step", "zn_ready", "zt_psum", "zt_ready", "wo_psum", "h2_ready"))
        c_norm, y2_ready, y2_psum, y2t_ready, gate_psum, pick_step, gap_ready, ex_ready = (sem(n) for n in (
            "c_norm", "y2_ready", "y2_psum", "y2t_ready", "gate_psum", "pick_step", "gap_ready", "ex_ready"))
        picked_ready, before_chain, before_ready, rank_psum, slot_ready, slot_step = (
            sem(n) for n in ("picked_ready", "before_chain", "before_ready", "rank_psum", "slot_ready", "slot_step"))
        slotu_ready, w_step, w_put, rows_filled, dest_next, rows_sent = (sem(n) for n in (
            "slotu_ready", "w_step", "w_put", "rows_filled", "dest_next", "rows_sent"))

        def wait(eng, s, v):
            if isinstance(v, int) and v <= 0:
                return
            eng.wait_ge(s, v)

        def passed_by(eng):
            eng.sem_inc(waits_passed, 1)

        def ago(s, i, q, d):
            return s[(q - d) % 2], i * (QB // 2) + (q - d) // 2 + 1

        def bc(ap, n):
            return ap.unsqueeze(len(ap.shape)).broadcast_to([*ap.shape, n])

        block = ctx.enter_context(nc.Block())
        n_const = [0]
        DVE_CONSTS = 10
        pool_steps = [0]

        @block.sync
        def _(sp):
            def load(dst, src):
                sp.dma_start(dst, src).then_inc(consts_loaded, 16)
                n_const[0] += 16

            def row(ap):
                return ap.rearrange("(a n) -> a n", a=1)

            def col(ap):
                return ap.rearrange("(n a) -> n a", a=1)

            def group(g):
                wait(sp, masked, g)
                for par in range(2):
                    for dst, src in ((rel_sb, rel), (adj_sb, adj)):
                        sp.dma_start(
                            dst[par * HALF:(par + 1) * HALF, :, :],
                            src[bass.ds(g * GB, GB), par::2, :].rearrange("b t j -> t b j"),
                        ).then_inc(pair_loaded, 16)
                wait(sp, onehot_ready, g)
                sp.dma_start(ids_sb[:], ids[bass.ds(g * GB, GB), :].rearrange("b (a t) -> a b t", a=1)
                             .broadcast_to([NA, GB, P])).then_inc(ids_loaded, 16)

            sp.wait_ge(pool_const, 3)
            load(both_embed[:, 0:D], atom_embed)
            load(both_embed[:, D:2 * D], neighbor_embed)
            load(wrd_col[D:2 * D, :], col(w_rd))
            load(w1_bd[0:D, 0:D], w1[0:D, :])
            load(w1_bd[D:2 * D, D:2 * D], w1[D:2 * D, :])
            load(b1_bc[:], row(b1).broadcast_to([NA, D]))
            for i in range(2):
                load(film[i * D:(i + 1) * D, 0:1], col(gamma))
                load(film[i * D:(i + 1) * D, 1:2], col(beta))
                load(w2_bd[i * D:(i + 1) * D, i * D:(i + 1) * D], w2)
                load(gate_bd[i * D:(i + 1) * D, i * NE:(i + 1) * NE], gate_w)
            load(b2_bc[:], row(b2).broadcast_to([P, D]))
            for i, (w, b) in enumerate(((W_Q, b_Q), (W_K, b_K), (W_V, b_V))):
                load(qkv_raw[:, i, :].rearrange("m (h d) -> m h d", h=H), w.rearrange("h m d -> m h d"))
                for c in range(2):
                    load(bias_col[:, i, c:c + 1], col(b.rearrange("h d -> (h d)"))[c * P:(c + 1) * P, :])
            load(wo_sb[:], W_O.rearrange("(c h) d m -> (h d) c m", c=2))
            load(bo_bc[:], row(b_O).broadcast_to([P, D]))
            load(gateb_bc[:], row(gate_b).broadcast_to([P, NE]))
            group(0)
            for i, w in enumerate((ew1, ew2)):
                load(ew12[:].rearrange("d (e i h) -> d i e h", e=NE, i=2)[:, i, :, :], w.rearrange("e d h -> d e h"))
            load(ew3_sb[:].rearrange("h (e o) -> h e o", e=NE), ew3.rearrange("e h o -> h e o"))
            load(sorted_rows[NE * REG:NE * REG + NE * P, :].rearrange("(i p) r -> p i r", p=P), pads[:, NE:2 * NE, :])
            with sp.Fori(1, NG) as g:
                group(g)

            wait(sp, tail_ready, 1)
            for e in range(NE):
                r = sp.value_load(tail_row[0:1, e:e + 1], min_val=0, max_val=NE * REG - P)
                sp.dma_start(sorted_rows[bass.ds(r, P), :], pads[:, e, :]).then_inc(pads_written, 16)
            wait(sp, pads_written, 16 * NE)
            wait(sp, rows_sent, 128 * NG)
            wait(sp, table_ready, 1)

            def load_rows(i):
                for q in range(QB):
                    wait(sp, rows_out[q], i * 64)
                    for u in range(4):
                        r = sp.value_load(tile_table[0:1, bass.ds(i * (4 * QB) + 4 * q + u, 1)],
                                          min_val=0, max_val=NE * REG + (NE - 1) * P)
                        sp.dma_start(x_rows[:, q, u, :], sorted_rows[bass.ds(r, P), :]).then_inc(x_loaded[q], 16)

            load_rows(0)
            with sp.Fori(1, NQ // QB) as i:
                load_rows(i)

            for q in range(QB):
                wait(sp, rows_out[q], 64 * (NQ // QB))
            for c in range(NCH):
                for k in range(TOPK):
                    sp.dma_start(picked_out[:, k, c * CB:(c + 1) * CB, :],
                                 expert_out[k * NTOK:(k + 1) * NTOK, :].rearrange("(p b) f -> p b f", b=NB)[
                                     :, c * CB:(c + 1) * CB, :]).then_inc(y_loaded[c], 16)
            for c in range(NCH):
                wait(sp, out_ready, c + 1)
                for par in range(2):
                    sp.dma_start(out[c * CB:(c + 1) * CB, par::2, :].rearrange("b t f -> t b f"),
                                 resid[par * HALF:(par + 1) * HALF, c * CB:(c + 1) * CB, :]).then_inc(stored, 16)
            sp.wait_ge(stored, 32 * NCH)

        CONSTS = n_const[0]

        @block.gpsimd
        def _(pool):
            n = 0

            def step(ins):
                nonlocal n
                n += 1
                ins.then_inc(pool_const, 1)
                pool.wait_ge(pool_const, n)

            for t in (w1_bd, w2_bd, gate_bd, wrd_col):
                pool.memset(t[:], 0.0 if t is not wrd_col else 1.0)
            step(pool.memset(a_bd[:], 0.0))
            step(pool.memset(pads[:], 0.0))
            step(pool.iota(pads[:, :, D + 1:D + 2].bitcast(I32), pattern=[[P, 2 * NE], [0, 1]], base=DUMP,
                           channel_multiplier=1))
            step(pool.memset(ident[:], 0.0))
            step(pool.affine_select(out=ident[:], in_=ident[:], compare_op=ALU.not_equal, fill=1.0, base=0,
                                    pattern=[[-1, P]], channel_multiplier=1))
            step(pool.memset(off_diag[:], 1.0))
            step(pool.affine_select(out=off_diag[:], in_=off_diag[:], compare_op=ALU.not_equal, fill=0.0,
                                    base=0, pattern=[[-1, P]], channel_multiplier=1))
            step(pool.tensor_copy(ident_b[:], ident[:]))
            step(pool.memset(causal[:], 0.0))
            step(pool.affine_select(out=causal[0:HALF, :].rearrange("p (h k) -> p h k", h=H),
                                    in_=causal[0:HALF, :].rearrange("p (h k) -> p h k", h=H),
                                    compare_op=ALU.is_gt, fill=-BIG, base=0,
                                    pattern=[[0, H], [-1, HALF]], channel_multiplier=1))
            step(pool.affine_select(out=causal[HALF:P, :].rearrange("p (h k) -> p h k", h=H),
                                    in_=causal[HALF:P, :].rearrange("p (h k) -> p h k", h=H),
                                    compare_op=ALU.is_ge, fill=-BIG, base=0,
                                    pattern=[[0, H], [-1, HALF]], channel_multiplier=1))
            step(pool.memset(eps_col[:], EPS))
            step(pool.memset(before[:], 1.0))
            step(pool.affine_select(out=before[:], in_=before[:], compare_op=ALU.is_gt, fill=0.0, base=0,
                                    pattern=[[1, P]], channel_multiplier=-1))
            step(pool.memset(ones_b[:], 1.0))
            step(pool.memset(head_sum[:], 1.0))
            for cmp_base, sign in ((0, 1), (DH - 1, -1)):
                step(pool.affine_select(out=head_sum[:], in_=head_sum[:], compare_op=ALU.is_ge, fill=0.0,
                                        base=cmp_base, pattern=[[-sign * DH, 4]], channel_multiplier=sign))
            step(pool.iota(tmp_i[:, 0:1], pattern=[[0, 1]], base=0, channel_multiplier=1))
            step(pool.tensor_copy(atom_no[:], tmp_i[:, 0:1]))
            step(pool.iota(tmp_i[:, 32:34], pattern=[[P, 2]], base=0, channel_multiplier=1))
            step(pool.tensor_copy(tile_no[:], tmp_i[:, 32:34]))
            step(pool.iota(tmp_i[:, 16:32], pattern=[[-1, NE]], base=NE, channel_multiplier=0))
            step(pool.tensor_copy(rev_e[:], tmp_i[:, 16:32]))
            step(pool.tensor_scalar(base_e[:], rev_e[:], -float(REG), float(NE * REG), ALU.mult, ALU.add))
            step(pool.iota(dest[:], pattern=[[NTOK, 2], [1, GB]], base=0, channel_multiplier=NB))
            step(pool.memset(y_tok[:, :, D - 1:D], 1.0))
            step(pool.memset(v_odd[:], 0.0))
            for par in range(2):
                step(pool.memset(v_odd[par * HALF:(par + 1) * HALF, :, :, par, DH:DH + 1], 1.0))
            step(pool.memset(picked_all[:], 0.0))
            pool_steps[0] = n


            def mask(g):
                wait(pool, pair_loaded, (g + 1) * 64)
                wait(pool, transposed_w, g)
                passed_by(pool)
                pool.tensor_copy(adj_f[:], adj_sb[:]).then_inc(adj_ready, 1)
                pool.wait_ge(adj_ready, g + 1)
                pool.tensor_tensor(
                    weighted[:].rearrange("p b (two t) -> p b two t", two=2),
                    rel_sb[:].rearrange("p b (t two) -> p b two t", two=2),
                    adj_f[:].rearrange("p b (t two) -> p b two t", two=2), ALU.mult).then_inc(masked, 1)
                wait(pool, ids_loaded, (g + 1) * 16)
                wait(pool, nb_psum, g)
                passed_by(pool)
                pool.tensor_scalar(
                    one_hot[:].rearrange("p b (two t) -> p b two t", two=2),
                    ids_sb[:].rearrange("p b (t two) -> p b two t", two=2),
                    atom_no[0:NA, :], None, ALU.is_equal).then_inc(onehot_ready, 1)

            def set_resid(g):
                wait(pool, h_ready, g + 1)
                pool.tensor_tensor(resid[:, bass.ds(g * GB, GB), :], h_tok[:],
                                   bo_bc[:].unsqueeze(1).broadcast_to([P, GB, D]), ALU.add).then_inc(resid_set, 1)

            def route(g):
                wait(pool, picked_ready, g + 1)
                wait(pool, before_ready, g)
                passed_by(pool)
                pool.tensor_copy(picked_before[:, 0, :], picked_all[:]).then_inc(before_chain, 1)
                for b in range(1, GB):
                    wait(pool, before_chain, g * GB + b)
                    pool.tensor_tensor(picked_before[:, b, :], picked_before[:, b - 1, :], picked[:, b - 1, :],
                                       ALU.add).then_inc(before_chain, 1)
                wait(pool, before_chain, g * GB + GB)
                pool.tensor_tensor(picked_all[:], picked_before[:, GB - 1, :], picked[:, GB - 1, :],
                                   ALU.add).then_inc(before_ready, 1)
                wait(pool, y2_ready, g + 1)
                wait(pool, rows_sent, g * 128)
                passed_by(pool)
                for k in range(2):
                    pool.tensor_copy(rows[:, k, :, 0:D], y2[:])
                pool.tensor_copy(rows[:, :, :, D + 1:D + 2].bitcast(U32),
                                 dest[:].unsqueeze(3)).then_inc(rows_filled, 1)
                pool.wait_ge(rows_filled, g + 1)
                passed_by(pool)
                pool.tensor_scalar(dest[:], dest[:], float(GB), None, ALU.add).then_inc(dest_next, 1)

            def send(g, first, last):
                if first == 0:
                    wait(pool, w_put, g + 1)
                    wait(pool, slotu_ready, g + 1)
                    wait(pool, dest_next, g + 1)
                    passed_by(pool)
                for i in range(first, last):
                    b, k = i // 2, i % 2
                    pool.indirect_dma_start(
                        sorted_rows, bass.IndirectOffsetOnAxis(ap=slot_u[:, k, b:b + 1], axis=0),
                        rows[:, k, b, :], None).then_inc(rows_sent, 16)

            def body(g, first=False):
                mask(g + 1)
                if not first:
                    send(g - 1, 0, 3)
                if not first:
                    send(g - 1, 3, 6)
                set_resid(g + 1)
                if not first:
                    send(g - 1, 6, 8)
                route(g)

            mask(0)
            set_resid(0)
            body(0, first=True)
            with pool.Fori(1, NG - 1) as g:
                body(g)
            send(NG - 2, 0, 8)
            route(NG - 1)
            send(NG - 1, 0, 8)

            with pool.Fori(0, NQ // QB) as i:
                for q in range(QB):
                    wait(pool, *ago(o_ready, i, q, 0))
                    passed_by(pool)
                    for u in range(4):
                        pool.indirect_dma_start(
                            expert_out,
                            bass.IndirectOffsetOnAxis(ap=x_rows[:, q, u, D + 1:D + 2].bitcast(U32), axis=0),
                            y_rows[:, q, u, :], None).then_inc(rows_out[q], 16)

        PC = pool_steps[0]

        @block.tensor
        def _(pe):
            n = 0

            def mm(out, lhsT, rhs, start=True, stop=True):
                return pe.matmul(out, lhsT, rhs, start=start, stop=stop, skip_group_check=True)

            pe.wait_ge(consts_loaded, CONSTS)
            pe.wait_ge(pool_const, PC)
            pe.transpose(ps_tok[:, 0:NA], both_embed[:], ident[0:NA, 0:NA]).then_inc(pe_const, 1)
            for i in range(3):
                for c in range(2):
                    last = pe.transpose(ps_pt[:, (i * 2 + c) * D:(i * 2 + c + 1) * D],
                                        qkv_raw[:, i, c * P:(c + 1) * P], ident[0:D, 0:D])
            last.then_inc(pe_const, 1)
            pe.wait_ge(dve_const, 1)
            mm(ps_g0[0:NA, 0:2 * D], embed_t[:], w1_bd[:]).then_inc(pe_const, 1)
            pe.wait_ge(dve_const, 2)
            for i in range(3):
                for c in range(2):
                    dst = (ps_tok if i < 2 else ps_g1)[:, (i % 2 * 2 + c) * P:(i % 2 * 2 + c + 1) * P]
                    last = pe.transpose(dst, qkv_t[:, i, c, :, :].rearrange("p a f -> p (a f)"), ident[:])
            last.then_inc(pe_const, 1)
            a_banks = [ps_scores[:, 0, :], ps_scores[:, 1, :], ps_z[:, 0, :], ps_z[:, 1, :]]
            for h in range(H):
                r, c = h % 4, h // 4
                at = slice(r * DH, (r + 1) * DH)
                last = mm(a_banks[r][:, c * D:(c + 1) * D],
                          qkv_t[at, 1, c, :, :].rearrange("p a f -> p (a f)"), qkv_t[at, 0, c, 0, :],
                          start=(c == 0))
            last.then_inc(pe_const, 1)

            def tok_weighted(g):
                wait(pe, masked, g + 1)
                wait(pe, v_ready[2], g)
                for b in range(GB):
                    last = pe.transpose(ps_g0[:, b * P:(b + 1) * P], weighted[:, b, :], ident[:])
                last.then_inc(transposed_w, 1)

            def tok_embed(g):
                wait(pe, onehot_ready, g + 1)
                wait(pe, slot_ready, g - 1)
                for b in range(GB):
                    for part in range(3):
                        last = mm(ps_tok[:, b * P:(b + 1) * P], one_hot[:, b, :], table_b[:, part, :],
                                  start=(b == 0 and part == 0))
                last.then_inc(nb_psum, 1)

            def tok_neighbors(g):
                wait(pe, wt_ready, g + 1)
                wait(pe, nb_ready, g + 1)
                for b in range(GB):
                    last = mm(ps_tok[:, b * P:b * P + D], weighted_t[:, b, :], nbr[:, b, :], start=False)
                last.then_inc(tok_psum, 1)

            def pair_transposes(dst, src):
                for p in range(NP):
                    last = pe.transpose(dst[:, p * P:(p + 1) * P],
                                        src[:, 2 * p:2 * p + 2, :].rearrange("p b f -> p (b f)"), ident[:])
                return last

            def tok_z(g):
                wait(pe, z_ready, g + 1)
                pair_transposes(ps_g0, z_tok).then_inc(z_psum, 1)

            def tok_w2(g):
                wait(pe, hs_ready, g + 1)
                for p in range(NP):
                    last = mm(ps_tok[:, p * P:(p + 1) * P], hs[:, p, :], w2_bd[:], start=(p == 0))
                last.then_inc(w2_psum, 1)

            def att_y(g):
                wait(pe, y_ready, g + 1)
                pair_transposes(ps_g0, y_tok).then_inc(y_psum, 1)

            def project(g):
                wait(pe, yt_ready, g + 1)
                for i in range(2):
                    if i == 1:
                        wait(pe, v_ready[3], g)
                    for h in range(4):
                        last = mm(ps_g[i][:, h * P:(h + 1) * P], a_bd[:, 4 * i + h, :], y_t[:, :, HALF:P],
                                  start=(h == 0))
                    last.then_inc(g_psum[i], 1)
                for par in range(2):
                    at = slice(par * D, (par + 1) * D)
                    wait(pe, g_ready[par], g + 1)
                    for i in range(2):
                        for c in range(2):
                            last = mm(ps_g[par][:, (2 * i + c) * P:(2 * i + c + 1) * P],
                                      qkv_w[at, i, c * P:(c + 1) * P], y_t[at, :, 0:HALF],
                                      start=(i + c == 0))
                    last.then_inc(qk_psum[par], 1)
                for b in range(GB):
                    p, par = b // 2, b % 2
                    at = slice(par * D, (par + 1) * D)
                    if p == 0:
                        wait(pe, prod_ready[par], g + 1)
                    else:
                        wait(pe, v_ready[par], g + 1)
                    mm(ps_g[par][:, 0:2 * P], y_t[at, p, HALF:HALF + P], qkv_w[at, 2, :])
                    mm(ps_g[par][0:HALF, 2 * P:4 * P], y_t[at, p, 0:HALF], qkv_w[at, 2, :],
                       start=False).then_inc(v_psum[b], 1)
                for par in range(2):
                    wait(pe, prod_ready[par], g + 1)
                    for p in range(NP):
                        for c in range(2):
                            col = (2 * p + par) * H + 4 * c
                            last = mm(ps_pt[0:HALF, col:col + 4], qk_prod[:, par, c, p * HALF:(p + 1) * HALF],
                                      head_sum[:], start=(par + p + c == 0))
                last.then_inc(diag_psum, 1)

            def scores(g, p):
                if p == 0:
                    wait(pe, sub_ready[1], g)
                    wait(pe, g_ready[0], g + 1)
                    wait(pe, g_ready[1], g + 1)
                else:
                    wait(pe, sub_ready[0], g + 1)
                for par in range(2):
                    at = slice(par * D, (par + 1) * D)
                    mm(ps_scores[:, par, :], ident_b[:], causal[:], stop=False)
                    last = mm(ps_scores[:, par, :], y_t[at, p, 0:P], g_sb[at, :, p, :], start=False)
                last.then_inc(s_psum[p], 1)

            def attend(g, p):
                wait(pe, p_ready[p], g + 1)
                if p == 0:
                    wait(pe, diag_ready, g + 1)
                else:
                    wait(pe, zt_ready[0], g + 1)
                for par in range(2):
                    b = 2 * p + par
                    if par == 1:
                        wait(pe, pt_ready[b - 1], g + 1)
                    for j in range(4):
                        last = pe.transpose(ps_pt[:, j * P:(j + 1) * P], probs[:, p, par, j * P:(j + 1) * P],
                                            ident[:])
                    last.then_inc(pt_psum[b], 1)
                    wait(pe, pt_ready[b], g + 1)
                    wait(pe, v_ready[b], g + 1)
                    if par == 0:
                        if p == 0:
                            wait(pe, h2_ready[1], g)
                        else:
                            wait(pe, h2_ready[0], g + 1)
                    w = 2 * (DH + 1)
                    for j in range(4):
                        last = mm(ps_z[:, par, j * w:(j + 1) * w], probs_t[:, par, j, :],
                                  v_odd[:, b, j, :, :], start=(j == 0))
                    last.then_inc(z_done[b], 1)

            def project_out(g, p):
                wait(pe, zn_ready[p], g + 1)
                for par in range(2):
                    for c in range(2):
                        last = pe.transpose(ps_pt[:, (2 * par + c) * P:(2 * par + c + 1) * P],
                                            zn[:, par * H + 4 * c:par * H + 4 * c + 4, :], ident[:])
                last.then_inc(zt_psum[p], 1)
                wait(pe, zt_ready[p], g + 1)
                for par in range(2):
                    for c in range(2):
                        last = mm(ps_z[:, 0, 384 + par * D:384 + (par + 1) * D], zt[:, par, c, :], wo_sb[:, c, :],
                                  start=(par + c == 0))
                last.then_inc(wo_psum[p], 1)

            def gate(g):
                wait(pe, y2_ready, g + 1)
                pair_transposes(ps_tok, y2).then_inc(y2_psum, 1)
                wait(pe, y2t_ready, g + 1)
                for p in range(NP):
                    last = mm(ps_tok[:, 256 + 2 * NE * p:256 + 2 * NE * (p + 1)], y2_t[:, p, :], gate_bd[:],
                              start=(p == 0))
                last.then_inc(gate_psum, 1)
                wait(pe, picked_ready, g + 1)
                wait(pe, before_ready, g + 1)
                mm(ps_tok[:, 384:384 + GB * NE], before[:], picked[:].rearrange("p b e -> p (b e)"))
                mm(ps_tok[:, 384:384 + GB * NE], ones_b[:], picked_before[:].rearrange("p b e -> p (b e)"),
                   start=False).then_inc(rank_psum, 1)

            pe.wait_ge(dve_const, DVE_CONSTS)
            pe.wait_ge(act_const, 1)
            tok_weighted(0)
            tok_embed(0)
            tok_neighbors(0)
            tok_z(0)
            tok_w2(0)
            att_y(0)
            project(0)
            def body(g):
                scores(g, 0)
                tok_weighted(g + 1)
                tok_embed(g + 1)
                tok_neighbors(g + 1)
                scores(g, 1)
                tok_z(g + 1)
                attend(g, 0)
                tok_w2(g + 1)
                project_out(g, 0)
                attend(g, 1)
                att_y(g + 1)
                project_out(g, 1)
                project(g + 1)
                gate(g)

            body(0)
            with pe.Fori(1, NG - 1) as g:
                body(g)
            g = NG - 1
            scores(g, 0)
            scores(g, 1)
            attend(g, 0)
            project_out(g, 0)
            attend(g, 1)
            project_out(g, 1)
            gate(g)

            wait(pe, slot_ready, NG)
            mm(ps_tok[:, 0:NE], ones_b[:], picked_all[:]).then_inc(cnt_psum, 1)
            wait(pe, dve_route, 1)
            for j in range(4):
                last = mm(ps_pt[0:1, j * P:(j + 1) * P], tile_vals[:, j:j + 1], ident[:], start=(j == 0))
            last.then_inc(table_psum, 1)
            wait(pe, table_ready, 1)

            def expert_of(i, q):
                return [pe.value_load(tile_table[0:1, bass.ds(2 * P + i * (4 * QB) + 4 * q + u, 1)],
                                      min_val=0, max_val=NE - 1) for u in range(4)]

            def turn(i, q):
                wait(pe, x_loaded[q], (i + 1) * 64)
                wait(pe, *ago(xt_ready, i, q, 1))
                passed_by(pe)
                for u in range(4):
                    last = pe.transpose(ps_g0[0:D, u * P:(u + 1) * P], x_rows[:, q, u, 0:D], ident[:])
                last.then_inc(xt_psum[q % 2], 1)

            def up(i, q):
                wait(pe, *ago(xt_ready, i, q, 0))
                wait(pe, *ago(hid_ready, i, q, 2))
                passed_by(pe)
                bank = (ps_scores, ps_z)[q % 2]
                for u, e in enumerate(expert_of(i, q)):
                    last = mm(bank[:, u // 2, u % 2 * 2 * HID:(u % 2 + 1) * 2 * HID], x_t[:, q % 2, u, :],
                              ew12[:, bass.ds(e * (2 * HID), 2 * HID)], start=(u % 2 == 0))
                last.then_inc(up_psum[q % 2], 1)

            def turn_hidden(i, q):
                wait(pe, *ago(hid_ready, i, q, 0))
                wait(pe, *ago(ht_ready, i, q, 1))
                for u in range(4):
                    last = pe.transpose(ps_g1[:, u * P:(u + 1) * P], hidden[:, q % 2, u, :], ident[:])
                last.then_inc(ht_psum[q % 2], 1)

            def down(i, q):
                wait(pe, *ago(ht_ready, i, q, 0))
                wait(pe, *ago(o_ready, i, q, 2))
                passed_by(pe)
                for u, e in enumerate(expert_of(i, q)):
                    last = mm((ps_tok, ps_pt)[q % 2][:, u * D:(u + 1) * D], hidden_t[:, q % 2, u, :],
                              ew3_sb[:, bass.ds(e * D, D)], start=(u == 0))
                last.then_inc(down_psum[q % 2], 1)

            def round_(i, first=False, last=False):
                for q in range(QB):
                    if q + 1 < QB:
                        turn(i, q + 1)
                    elif not last:
                        turn(i + 1, 0)
                    if q:
                        turn_hidden(i, q - 1)
                    elif not first:
                        turn_hidden(i - 1, QB - 1)
                    up(i, q)
                    if q:
                        down(i, q - 1)
                    elif not first:
                        down(i - 1, QB - 1)

            N = NQ // QB
            turn(0, 0)
            round_(0, first=True)
            with pe.Fori(1, N - 1) as i:
                round_(i)
            round_(N - 1, last=True)
            turn_hidden(N - 1, QB - 1)
            down(N - 1, QB - 1)

        @block.scalar
        def _(act):
            act.wait_ge(pe_const, 5)
            act.wait_ge(pool_const, PC)
            for r in range(4):
                bank = (ps_scores if r < 2 else ps_z)[:, r % 2, 0:2 * D]
                for i in range(2):
                    at = slice(i * D, (i + 1) * D)
                    last = act.activation(a_bd[at, r::4, i * D:(i + 1) * D],
                                          bank[at, :].rearrange("p (c f) -> p c f", c=2), ACT.Copy)
            last.then_inc(act_const, 1)
            act.wait_ge(dve_const, DVE_CONSTS)

            def tok_nbr(g):
                wait(act, nb_psum, g + 1)
                wait(act, tok_psum, g)
                act.activation(nbr[:], ps_tok[:].rearrange("p (b f) -> p b f", b=GB)[:, :, D:2 * D],
                               ACT.Copy).then_inc(nb_ready, 1)

            def rstd(g, mv, rs, stats, ready):
                wait(act, stats, g + 1)
                act.activation(rs[:, 0, :], mv[:, :, 1], ACT.Ln, bias=eps_col[:]).then_inc(ready, 1)
                wait(act, ready, g * 2 + 1)
                act.activation(rs[:, 1, :], rs[:, 0, :], ACT.Exp, scale=-0.5).then_inc(ready, 1)

            def tok_exp(g):
                wait(act, z_psum, g + 1)
                wait(act, hs_ready, g)
                act.activation(en[:].rearrange("p c t -> p (c t)"), ps_g0[:, 0:2 * P], ACT.Exp,
                               scale=film[:, 2:3], bias=film[:, 3:4]).then_inc(exp_ready, 1)

            def att_yt(g):
                wait(act, y_psum, g + 1)
                wait(act, s_psum[1], g)
                src = ps_g0[:, 0:2 * P].rearrange("p (c t) -> p c t", c=NP)
                act.activation(y_t[:, :, 0:P], src, ACT.Copy)
                act.activation(y_t[:, :, P:P + HALF], src[:, :, HALF:P], ACT.Copy).then_inc(yt_ready, 1)

            def project(g):
                for i in range(2):
                    wait(act, g_psum[i], g + 1)
                    act.activation(g_sb[:, 4 * i:4 * i + 4, :, :].rearrange("p h c k -> p (h c k)"),
                                   ps_g[i][:], ACT.Copy).then_inc(g_ready[i], 1)
                for par in range(2):
                    wait(act, qk_psum[par], g + 1)
                    wait(act, prod_ready[par], g)
                    act.activation(k_even[:, par, :, :].rearrange("p c t -> p (c t)"),
                                   ps_g[par][:, 2 * P:4 * P], ACT.Copy).then_inc(ke_ready[par], 1)
                for b in range(GB):
                    par = b % 2
                    wait(act, v_psum[b], g + 1)
                    wait(act, z_done[b], g)
                    for i in range(2):
                        at = slice(i * HALF, (i + 1) * HALF)
                        act.activation(v_odd[at, b, :, i, 0:DH],
                                       ps_g[par][at, 0:2 * P].rearrange("p (j i d) -> p j i d", i=2, d=DH)[:, :, i, :],
                                       ACT.Copy)
                    wait(act, z_step[b // 2], g * 6)
                    act.activation(v_even[:, b, :, :].rearrange("p h d -> p (h d)"),
                                   ps_g[par][0:HALF, 2 * P:4 * P], ACT.Copy).then_inc(v_ready[b], 1)

            def softmax(g, p):
                wait(act, sub_ready[p], g + 1)
                q = probs[:, p, :, :].rearrange("p c k -> p (c k)")
                act.activation(q, q, ACT.Exp).then_inc(p_ready[p], 1)
                wait(act, dsub_ready[p], g + 1)
                act.activation(p_diag[:, p, :], p_diag[:, p, :], ACT.Exp).then_inc(pd_ready[p], 1)

            def attend(g, p):
                for par in range(2):
                    b = 2 * p + par
                    wait(act, pt_psum[b], g + 1)
                    if p == 1:
                        wait(act, z_done[par], g + 1)
                    act.activation(probs_t[:, par, :, :].rearrange("p j t -> p (j t)"), ps_pt[:], ACT.Copy)\
                       .then_inc(pt_ready[b], 1)

            def project_out(g, p):
                wait(act, zt_psum[p], g + 1)
                act.activation(zt[:].rearrange("p b c t -> p (b c t)"), ps_pt[:], ACT.Copy).then_inc(zt_ready[p], 1)

            def gate(g):
                rstd(g, mv_c, rs_c, c_stats, c_rstd)
                wait(act, y2_psum, g + 1)
                act.activation(y2_t[:].rearrange("p c t -> p (c t)"), ps_tok[:, 0:2 * P], ACT.Copy)\
                   .then_inc(y2t_ready, 1)
                wait(act, gap_ready, g + 1)
                act.activation(ex[:], dmx[:], ACT.Exp).then_inc(ex_ready, 1)

            tok_nbr(0)
            rstd(0, mv_a, rs_a, a_stats, a_rstd)
            tok_exp(0)
            rstd(0, mv_b, rs_b, b_stats, b_rstd)
            att_yt(0)
            project(0)
            def body(g):
                tok_nbr(g + 1)
                softmax(g, 0)
                rstd(g + 1, mv_a, rs_a, a_stats, a_rstd)
                softmax(g, 1)
                tok_exp(g + 1)
                attend(g, 0)
                project_out(g, 0)
                rstd(g + 1, mv_b, rs_b, b_stats, b_rstd)
                attend(g, 1)
                att_yt(g + 1)
                project_out(g, 1)
                project(g + 1)
                gate(g)

            body(0)
            with act.Fori(1, NG - 1) as g:
                body(g)
            g = NG - 1
            softmax(g, 0)
            softmax(g, 1)
            attend(g, 0)
            project_out(g, 0)
            attend(g, 1)
            project_out(g, 1)
            gate(g)

            def turned(i, q):
                wait(act, *ago(xt_psum, i, q, 0))
                wait(act, *ago(up_psum, i, q, 2))
                act.activation(x_t[:, q % 2, :, :].rearrange("p u t -> p (u t)"), ps_g0[0:D, :], ACT.Copy)\
                   .then_inc(xt_ready[q % 2], 1)

            def turned_hidden(i, q):
                wait(act, *ago(ht_psum, i, q, 0))
                wait(act, *ago(down_psum, i, q, 2))
                act.activation(hidden_t[:, q % 2, :, :].rearrange("p u t -> p (u t)"), ps_g1[:], ACT.Copy)\
                   .then_inc(ht_ready[q % 2], 1)

            def gated(i, q):
                wait(act, *ago(up_psum, i, q, 0))
                wait(act, *ago(hid_ready, i, q, 2))
                h1 = (ps_scores, ps_z)[q % 2][:].rearrange("p c (u i h) -> p (c u) i h", u=2, i=2)[:, :, 0, :]
                act.activation(silu[:, q % 2, :, :], h1, ACT.Silu).then_inc(silu_ready[q % 2], 1)

            def round_(i, first=False, last=False):
                for q in range(QB):
                    if q + 1 < QB:
                        turned(i, q + 1)
                    elif not last:
                        turned(i + 1, 0)
                    if q:
                        turned_hidden(i, q - 1)
                    elif not first:
                        turned_hidden(i - 1, QB - 1)
                    gated(i, q)

            N = NQ // QB
            turned(0, 0)
            round_(0, first=True)
            with act.Fori(1, N - 1) as i:
                round_(i)
            round_(N - 1, last=True)
            turned_hidden(N - 1, QB - 1)

        @block.vector
        def _(dve):
            n = 0

            def step(ins):
                nonlocal n
                n += 1
                ins.then_inc(dve_const, 1)
                dve.wait_ge(dve_const, n)

            dve.wait_ge(consts_loaded, CONSTS)
            dve.wait_ge(pool_const, PC)
            dve.wait_ge(pe_const, 1)
            step(dve.tensor_scalar(embed_t[:], ps_tok[:, 0:NA], wrd_col[:], None, ALU.mult))
            dve.wait_ge(pe_const, 2)
            for i in range(3):
                s = SCALE if i == 0 else 1.0
                for c in range(2):
                    src = ps_pt[:, (i * 2 + c) * D:(i * 2 + c + 1) * D]
                    for a in range(2):
                        dve.tensor_scalar(qkv_t[:, i, c, a, 0:D - 1], src[:, 0:D - 1], src[:, D - 1:D], s,
                                          ALU.subtract, ALU.mult)
                        ins = dve.tensor_scalar(qkv_t[:, i, c, a, D - 1:D], bias_col[:, i, c:c + 1], s, None,
                                                ALU.mult)
            step(ins)
            dve.wait_ge(pe_const, 3)
            dve.tensor_copy(table[:, D:2 * D], ps_g0[0:NA, D:2 * D])
            step(dve.tensor_tensor(table[:, 0:D], ps_g0[0:NA, 0:D], b1_bc[:], ALU.add))
            step(dve.tensor_copy(table_b[:, 0, :], table[:]))
            step(dve.tensor_tensor(table_r[:], table[:], table_b[:, 0, :], ALU.subtract))
            step(dve.tensor_copy(table_b[:, 1, :], table_r[:]))
            step(dve.tensor_tensor(table[:], table_r[:], table_b[:, 1, :], ALU.subtract))
            step(dve.tensor_copy(table_b[:, 2, :], table[:]))
            step(dve.tensor_scalar(film[:, 2:4], film[:, 0:2], -1.0, None, ALU.mult))
            dve.wait_ge(pe_const, 4)
            for i in range(3):
                src = (ps_tok if i < 2 else ps_g1)[:, i % 2 * 2 * P:(i % 2 + 1) * 2 * P]
                ins = dve.tensor_copy(qkv_w[:, i, :], src)
            step(ins)
            assert n == DVE_CONSTS


            def norm(g, src, st, mv, rs, dst, width, sems, before=None):
                chain, stats, rstd, ready = sems
                for b in range(GB):
                    ins = dve.bn_stats(st[:, b, :], src(b))
                ins.then_inc(chain, 1)
                dve.wait_ge(chain, g + 1)
                passed_by(dve)
                for b in range(GB):
                    ins = dve.bn_aggr(mv[:, b, :], st[:, b, :])
                ins.then_inc(stats, 1)
                wait(dve, rstd, g * 2 + 2)
                if before:
                    before()
                for b in range(GB):
                    ins = dve.tensor_scalar(dst[:, b, 0:width], src(b)[:, 0:width], mv[:, b, 0:1], rs[:, 1, b:b + 1],
                                            ALU.subtract, ALU.mult)
                ins.then_inc(ready, 1)

            def tok_wt(g):
                wait(dve, transposed_w, g + 1)
                wait(dve, tok_psum, g)
                dve.tensor_tensor(weighted_t[:], ps_g0[:].rearrange("p (b t) -> p b t", b=GB),
                                  off_diag[:].unsqueeze(1).broadcast_to([P, GB, P]), ALU.mult).then_inc(wt_ready, 1)

            def tok_norm(g):
                wait(dve, tok_psum, g + 1)
                norm(g, lambda b: ps_tok[:, b * P:b * P + D], st_a, mv_a, rs_a, z_tok, D,
                     (a_norm, a_stats, a_rstd, z_ready), lambda: wait(dve, z_psum, g))

            def tok_silu(g):
                wait(dve, exp_ready, g + 1)
                dve.tensor_scalar(gz[:].rearrange("p c t -> p (c t)"), ps_g0[:, 0:2 * P], film[:, 0:1], film[:, 1:2],
                                  ALU.mult, ALU.add).then_inc(gz_ready, 1)
                dve.tensor_scalar(en1[:], en[:], 1.0, None, ALU.add).then_inc(gz_ready, 1)
                dve.wait_ge(gz_ready, g * 3 + 2)
                dve.reciprocal(en1[:], en1[:]).then_inc(gz_ready, 1)
                dve.wait_ge(gz_ready, g * 3 + 3)
                wait(dve, w2_psum, g)
                dve.tensor_tensor(hs[:], en1[:], gz[:], ALU.mult).then_inc(hs_ready, 1)

            def tok_h(g):
                wait(dve, w2_psum, g + 1)
                wait(dve, resid_set, g)
                dve.tensor_tensor(h_tok[:], ps_tok[:, 0:GB * D].rearrange("p (b f) -> p b f", b=GB),
                                  b2_bc[:].unsqueeze(1).broadcast_to([P, GB, D]), ALU.add).then_inc(h_ready, 1)
                dve.wait_ge(h_ready, g + 1)
                norm(g, lambda b: h_tok[:, b, :], st_b, mv_b, rs_b, y_tok, D - 1,
                     (b_norm, b_stats, b_rstd, y_ready), lambda: wait(dve, y_psum, g))

            def project(g):
                for par in range(2):
                    wait(dve, ke_ready[par], g + 1)
                    wait(dve, diag_psum, g)
                    dve.tensor_tensor(qk_prod[:, par, :, :].rearrange("p c t -> p (c t)"), ps_g[par][:, 0:2 * P],
                                      k_even[:, par, :, :].rearrange("p c t -> p (c t)"),
                                      ALU.mult).then_inc(prod_ready[par], 1)
                wait(dve, diag_psum, g + 1)
                wait(dve, dsub_ready[1], g)
                dve.tensor_copy(diag_s[:].rearrange("p b h -> p (b h)"), ps_pt[0:HALF, 0:GB * H])\
                   .then_inc(diag_ready, 1)

            def softmax(g, p):
                wait(dve, s_psum[p], g + 1)
                s = ps_scores[:].rearrange("p c (h k) -> p (c h) k", h=H)
                d = diag_s[:, 2 * p:2 * p + 2, :].rearrange("p b h -> p (b h)")
                dve.tensor_reduce(row_max[:, p, :], s, AXX, ALU.max).then_inc(max_step[p], 1)
                dve.wait_ge(max_step[p], g * 2 + 1)
                dve.wait_ge(diag_ready, g + 1)
                dve.tensor_tensor(row_max[0:HALF, p, :], row_max[0:HALF, p, :], d, ALU.max).then_inc(max_step[p], 1)
                dve.wait_ge(max_step[p], g * 2 + 2)
                wait(dve, pt_psum[2 * p + 1], g)
                dve.tensor_tensor(probs[:, p, :, :].rearrange("p c (h k) -> p (c h) k", h=H), s,
                                  bc(row_max[:, p, :], HALF), ALU.subtract).then_inc(sub_ready[p], 1)
                dve.tensor_tensor(p_diag[:, p, :], d, row_max[0:HALF, p, :], ALU.subtract).then_inc(dsub_ready[p], 1)

            def normalize(g, p):
                wait(dve, z_done[2 * p + 1], g + 1)
                w = DH + 1
                z = ps_z[:, :, 0:H * w].rearrange("p c (h w) -> p c h w", w=w)
                den_v = den[:].rearrange("p (c h) -> p c h", c=2)
                dve.tensor_copy(den_v, z[:, :, :, DH]).then_inc(z_step[p], 1)
                dve.wait_ge(z_step[p], g * 6 + 1)
                dve.wait_ge(pd_ready[p], g + 1)
                dve.tensor_tensor(den[0:HALF, :], den[0:HALF, :], p_diag[:, p, :], ALU.add).then_inc(z_step[p], 1)
                dve.wait_ge(z_step[p], g * 6 + 2)
                dve.reciprocal(rden[:], den[:]).then_inc(z_step[p], 1)
                dve.wait_ge(z_step[p], g * 6 + 3)
                dve.tensor_tensor(pdn[:], p_diag[:, p, :], rden[0:HALF, :], ALU.mult).then_inc(z_step[p], 1)
                if p == 0:
                    wait(dve, zt_psum[1], g)
                else:
                    wait(dve, zt_psum[0], g + 1)
                dve.tensor_tensor(zn[:].rearrange("p (c h) d -> p c h d", c=2), z[:, :, :, 0:DH],
                                  bc(rden[:].rearrange("p (c h) -> p c h", c=2), DH), ALU.mult).then_inc(z_step[p], 1)
                dve.wait_ge(z_step[p], g * 6 + 4)
                dve.tensor_tensor(pv_even[:], v_even[:, 2 * p:2 * p + 2, :, :].rearrange("p b h d -> p (b h) d"),
                                  bc(pdn[:], DH), ALU.mult).then_inc(z_step[p], 1)
                dve.wait_ge(z_step[p], g * 6 + 6)
                dve.wait_ge(z_step[p], g * 6 + 5)
                dve.tensor_tensor(zn[0:HALF, :, :], zn[0:HALF, :, :], pv_even[:], ALU.add).then_inc(zn_ready[p], 1)

            def add_attention(g, p):
                wait(dve, wo_psum[p], g + 1)
                wait(dve, resid_set, g + 1)
                r = resid[:, bass.ds(g * GB + 2 * p, 2), :]
                dve.tensor_tensor(r, ps_z[:, 0, 384:384 + 2 * D].rearrange("p (b f) -> p b f", b=2), r,
                                  ALU.add).then_inc(h2_ready[p], 1)

            def pick(g, k, src, at):
                dve.tensor_reduce(mx[:, k, :], src, AXX, ALU.max).then_inc(pick_step, 1)
                dve.wait_ge(pick_step, g * 12 + at + 1)
                dve.tensor_tensor(eq[:, k, :, :], src, bc(mx[:, k, :], NE), ALU.is_equal).then_inc(pick_step, 1)
                dve.wait_ge(pick_step, g * 12 + at + 2)
                rev = rev_e[:].unsqueeze(1).broadcast_to([P, GB, NE])
                dve.tensor_tensor(eq[:, k, :, :], eq[:, k, :, :], rev, ALU.mult).then_inc(pick_step, 1)
                dve.wait_ge(pick_step, g * 12 + at + 3)
                dve.tensor_reduce(rk[:, k, :], eq[:, k, :, :], AXX, ALU.max).then_inc(pick_step, 1)
                dve.wait_ge(pick_step, g * 12 + at + 4)
                dve.tensor_tensor(oh[:, k, :, :], rev, bc(rk[:, k, :], NE), ALU.is_equal).then_inc(pick_step, 1)
                dve.wait_ge(pick_step, g * 12 + at + 5)

            def gate(g):
                dve.wait_ge(h2_ready[1], g + 1)
                passed_by(dve)
                norm(g, lambda b: resid[:, bass.ds(g * GB + b, 1), :].rearrange("p b f -> p (b f)"),
                     st_c, mv_c, rs_c, y2, D, (c_norm, c_stats, c_rstd, y2_ready), lambda: wait(dve, rows_filled, g))
                wait(dve, gate_psum, g + 1)
                dve.tensor_tensor(lg[:], ps_tok[:, 256:256 + GB * NE].rearrange("p (b e) -> p b e", b=GB),
                                  gateb_bc[:].unsqueeze(1).broadcast_to([P, GB, NE]), ALU.add).then_inc(pick_step, 1)
                dve.wait_ge(pick_step, g * 12 + 1)
                pick(g, 0, lg[:], 1)
                dve.scalar_tensor_tensor(lg2[:], oh[:, 0, :, :], -3.0e38, lg[:], ALU.mult, ALU.add)\
                   .then_inc(pick_step, 1)
                dve.wait_ge(pick_step, g * 12 + 7)
                pick(g, 1, lg2[:], 7)
                wait(dve, rank_psum, g)
                dve.tensor_tensor(picked[:], oh[:, 0, :, :], oh[:, 1, :, :], ALU.add).then_inc(picked_ready, 1)
                dve.tensor_tensor(dmx[:], mx[:, 1, :], mx[:, 0, :], ALU.subtract).then_inc(gap_ready, 1)
                wait(dve, ex_ready, g + 1)
                dve.tensor_scalar(ex1[:], ex[:], 1.0, None, ALU.add).then_inc(w_step, 1)
                dve.wait_ge(w_step, g * 3 + 1)
                dve.reciprocal(wt[:, 0, :], ex1[:]).then_inc(w_step, 1)
                dve.wait_ge(w_step, g * 3 + 2)
                dve.tensor_tensor(wt[:, 1, :], wt[:, 0, :], ex[:], ALU.mult).then_inc(w_step, 1)
                dve.wait_ge(w_step, g * 3 + 3)
                wait(dve, rows_sent, g * 128)
                dve.tensor_copy(rows[:, :, :, D], wt[:]).then_inc(w_put, 1)
                wait(dve, rank_psum, g + 1)
                dve.tensor_tensor(slot[:], ps_tok[:, 384:384 + GB * NE].rearrange("p (b e) -> p b e", b=GB),
                                  base_e[:].unsqueeze(1).broadcast_to([P, GB, NE]), ALU.add).then_inc(slot_ready, 1)
                dve.wait_ge(slot_ready, g + 1)
                dve.tensor_tensor(slot2[:], oh[:], slot[:].unsqueeze(1).broadcast_to([P, 2, GB, NE]), ALU.mult)\
                   .then_inc(slot_step, 1)
                dve.wait_ge(slot_step, g * 2 + 1)
                dve.tensor_reduce(slot_f[:], slot2[:], AXX, ALU.add).then_inc(slot_step, 1)
                dve.wait_ge(slot_step, g * 2 + 2)
                dve.tensor_copy(slot_u[:], slot_f[:]).then_inc(slotu_ready, 1)

            tok_wt(0)
            tok_norm(0)
            tok_silu(0)
            tok_h(0)
            project(0)
            def body(g):
                softmax(g, 0)
                tok_wt(g + 1)
                tok_norm(g + 1)
                softmax(g, 1)
                tok_silu(g + 1)
                normalize(g, 0)
                tok_h(g + 1)
                add_attention(g, 0)
                normalize(g, 1)
                add_attention(g, 1)
                project(g + 1)
                gate(g)

            body(0)
            with dve.Fori(1, NG - 1) as g:
                body(g)
            g = NG - 1
            softmax(g, 0)
            softmax(g, 1)
            normalize(g, 0)
            add_attention(g, 0)
            normalize(g, 1)
            add_attention(g, 1)
            gate(g)

            def route(ins):
                nonlocal n
                n += 1
                ins.then_inc(dve_const, 1)
                dve.wait_ge(dve_const, n)

            wait(dve, cnt_psum, 1)
            route(dve.tensor_copy(count[:], ps_tok[:, 0:NE]))
            dve.tensor_tensor(tail_row[:], count[:], base_e[:], ALU.add).then_inc(tail_ready, 1)
            dve.memset(ones_e[:], 1.0)
            route(dve.tensor_scalar(cnt_r[:], count[:], float(P - 1), None, ALU.add))
            route(dve.tensor_scalar(cnt_m[:], cnt_r[:], 7, None, ALU.arith_shift_right))
            route(dve.tensor_copy(n_tiles[:], cnt_m[:]))
            route(dve.tensor_tensor_scan(tiles_to[:], ones_e[:], n_tiles[:], 0.0, ALU.mult, ALU.add))
            route(dve.tensor_tensor(past[:], tiles_to[:].unsqueeze(1).broadcast_to([P, 2, NE]), bc(tile_no[:], NE),
                                    ALU.is_le))
            route(dve.tensor_tensor(past_n[:], past[:], n_tiles[:].unsqueeze(1).broadcast_to([P, 2, NE]), ALU.mult))
            dve.tensor_reduce(tile_e[:], past[:], AXX, ALU.add)
            route(dve.tensor_reduce(tile_s[:], past_n[:], AXX, ALU.add))
            route(dve.tensor_tensor(tile_d[:], tile_no[:], tile_s[:], ALU.subtract))
            route(dve.tensor_scalar(tile_d[:], tile_d[:], float(P), None, ALU.mult))
            dve.scalar_tensor_tensor(tile_vals[:, 0:2], tile_e[:], float(REG), tile_d[:], ALU.mult, ALU.add)
            dve.tensor_scalar(tile_vals[:, 2:4], tile_e[:], float(NE - 1), None, ALU.min).then_inc(dve_route, 1)
            wait(dve, table_psum, 1)
            dve.tensor_copy(tile_table[:], ps_pt[0:1, :]).then_inc(table_ready, 1)

            def hid(i, q):
                wait(dve, *ago(silu_ready, i, q, 0))
                wait(dve, *ago(ht_psum, i, q, 2))
                h2 = (ps_scores, ps_z)[q % 2][:].rearrange("p c (u i h) -> p (c u) i h", u=2, i=2)[:, :, 1, :]
                dve.tensor_tensor(hidden[:, q % 2, :, :], silu[:, q % 2, :, :], h2, ALU.mult).then_inc(hid_ready[q % 2], 1)

            def weigh(i, q):
                wait(dve, *ago(down_psum, i, q, 0))
                wait(dve, rows_out[q], i * 64)
                bank = (ps_tok, ps_pt)[q % 2][:, 0:4 * D].rearrange("p (u f) -> p u f", u=4)
                dve.tensor_tensor(y_rows[:, q, :, :], bank, x_rows[:, q, :, D:D + 1].broadcast_to([P, 4, D]),
                                  ALU.mult).then_inc(o_ready[q % 2], 1)

            def round_(i, first=False):
                for q in range(QB):
                    hid(i, q)
                    if q:
                        weigh(i, q - 1)
                    elif not first:
                        weigh(i - 1, QB - 1)

            N = NQ // QB
            round_(0, first=True)
            with dve.Fori(1, N) as i:
                round_(i)
            weigh(N - 1, QB - 1)

            for c in range(NCH):
                at = slice(c * CB, (c + 1) * CB)
                wait(dve, y_loaded[c], 32)
                dve.tensor_tensor(resid[:, at, :], resid[:, at, :], picked_out[:, 0, at, :], ALU.add).then_inc(added, 1)
                dve.wait_ge(added, c + 1)
                dve.tensor_tensor(resid[:, at, :], resid[:, at, :], picked_out[:, 1, at, :], ALU.add)\
                   .then_inc(out_ready, 1)


_INS = ['x', 'mask_BSS_b0_1', 'fside_BSS_rel_dist', 'L0_tok_atom_embed', 'L0_tok_neighbor_embed', 'L0_tok_w_rd',
        'L0_tok_w1', 'L0_tok_b1', 'L0_tok_gamma', 'L0_tok_beta', 'L0_tok_w2', 'L0_tok_b2', 'L0_attn_W_Q',
        'L0_attn_W_K', 'L0_attn_W_V', 'L0_attn_W_O', 'L0_attn_b_Q', 'L0_attn_b_K', 'L0_attn_b_V', 'L0_attn_b_O',
        'L0_ffn_gate_w', 'L0_ffn_gate_b', 'L0_ffn_w1', 'L0_ffn_w2', 'L0_ffn_w3']


def program(nc, arrays):
    args = [nc.dram_tensor(f"in_{name}_dram", a.shape, mybir.dt.from_np(a.dtype), kind="ExternalInput").ap()
            for name, a in arrays.items()]
    NB, S = arrays['x'].shape
    NE, D, _ = arrays['L0_ffn_w1'].shape
    NTOK = NB * S
    out = nc.dram_tensor("out_0_dram", (NB, S, D), F32, kind="ExternalOutput").ap()
    sorted_rows = nc.dram_tensor("sorted_rows", (NE * (NTOK + P) + NE * P, D + 2), F32).ap()
    expert_out = nc.dram_tensor("expert_out", (2 * NTOK + 2 * NE * P, D), F32).ap()
    lm_tower_kernel(nc, *args, out, sorted_rows, expert_out)


def kernel(**inputs):
    import numpy as _np
    import concourse.bacc as _bacc
    from concourse.bass_utils import run_bass_kernel_spmd as _run

    nc = _bacc.Bacc("TRN2", target_bir_lowering=False, num_devices=1)
    arrays = {}
    for name in _INS:
        a = _np.ascontiguousarray(inputs[name])
        arrays[name] = a
    program(nc, arrays)
    r = _run(nc, [{f"in_{name}_dram": a for name, a in arrays.items()}], core_ids=[0])
    return r.results[0]["out_0_dram"]
```

```python
from contextlib import ExitStack

import concourse.bass as bass
from concourse import mybir

ALU = mybir.AluOpType
ACT = mybir.ActivationFunctionType
AXX = mybir.AxisListType.X
F32 = mybir.dt.float32
BF16 = mybir.dt.bfloat16
I32 = mybir.dt.int32
U32 = mybir.dt.uint32
F32R = mybir.dt.float32r

P = 128
HALF = P // 2
GB = 4
NP = 2
HIGH_BITS = 0xFFFFF000
BIG = 1.0e30
EPS = 1e-5
EXP_LN_SET = 6


def lm_tower_kernel(
    nc, ids, adj, rel, atom_embed, neighbor_embed, w_rd, w1, b1, gamma, beta, w2, b2,
    W_Q, W_K, W_V, W_O, b_Q, b_K, b_V, b_O, gate_w, gate_b, ew1, ew2, ew3,
    out, sorted_rows, expert_out,
):
    NB, S = ids.shape
    D = w2.shape[0]
    H, _, DH = W_Q.shape
    NA = atom_embed.shape[0]
    NE, _, HID = ew1.shape
    NG = NB // GB
    NTOK = NB * S
    REG = NTOK + P
    TOPK = 2
    NT = TOPK * NTOK // P + NE
    ROW = 2 * D + 2
    DUMP = TOPK * NTOK
    NQ = NT // 4
    QB = 6
    SCALE = float(DH) ** -0.5
    assert S == P and NQ <= HALF and D == HALF and H * DH == 2 * P and NG * GB == NB and NQ % QB == 0 and NE == 16 and NB * D <= NE * 2 * HID

    with ExitStack() as ctx:
        def sb(name, shape, dt=F32):
            return ctx.enter_context(nc.sbuf_tensor(name, shape, dt))

        def sem(name):
            return ctx.enter_context(nc.semaphore(name))

        psum = [ctx.enter_context(nc.psum_tensor(f"bank{i}", [P, 512], F32)) for i in range(4)]
        ps_scores = ctx.enter_context(nc.psum_tensor("ps_scores", [P, 2, 512], F32))
        ps_z = ctx.enter_context(nc.psum_tensor("ps_z", [P, 2, 512], F32))
        ps_tok, ps_pt, ps_g0, ps_g1 = psum
        ps_g = [ps_g0, ps_g1]

        ident = sb("ident", [P, P])
        ident_b = sb("ident_b", [P, P], BF16)
        off_diag = sb("off_diag", [P, P])
        causal = sb("causal", [P, 512], BF16)
        before = sb("before", [P, P], BF16)
        ones_b = sb("ones_b", [P, P], BF16)
        head_sum = sb("head_sum", [P, 4])
        atom_no = sb("atom_no", [P, 1])
        quad_of = sb("quad_of", [P, 32])
        rev_e = sb("rev_e", [P, NE])
        base_e = sb("base_e", [P, NE])
        dest = sb("dest", [P, 2, GB], I32)
        tmp_i = sb("tmp_i", [P, 64], I32)
        both_embed = sb("both_embed", [NA, 2 * D])
        embed_t = sb("embed_t", [P, NA])
        wrd_col = sb("wrd_col", [P, 1])
        w1_bd = sb("w1_bd", [P, 2 * D])
        b1_bc = sb("b1_bc", [NA, D])
        table = sb("table", [NA, 2 * D])
        table_r = sb("table_r", [NA, 2 * D])
        table_b = sb("table_b", [NA, 3, 2 * D], BF16)
        eps_col = sb("eps_col", [P, 1])
        film = sb("film", [P, 4])
        w2_bd = sb("w2_bd", [P, 2 * D])
        b2_bc = sb("b2_bc", [P, D])
        qkv_raw = sb("qkv_raw", [D, 3, H * DH])
        bias_col = sb("bias_col", [P, 3, 2])
        qkv_t = sb("qkv_t", [P, 3, 2, 2, D])
        qkv_w = sb("qkv_w", [P, 3, 2 * P])
        a_bd = sb("a_bd", [P, H, P])
        wo_sb = sb("wo_sb", [P, 2, D])
        bo_bc = sb("bo_bc", [P, D])
        gate_bd = sb("gate_bd", [P, 2 * NE])
        gateb_bc = sb("gateb_bc", [P, NE])
        ew12 = sb("ew12", [P, NE * 2 * HID])
        ew12_high = sb("ew12_high", [P, NE * 2 * HID])
        WS = NE * 2 * HID // NG
        high_u = sb("high_u", [P, WS], U32)
        ew3_sb = sb("ew3_sb", [HID, NE * D])
        rel_sb = sb("rel_sb", [P, GB, P])
        adj_sb = sb("adj_sb", [P, GB, P], mybir.dt.uint8)
        adj_f = sb("adj_f", [P, GB, P])
        ids_sb = sb("ids_sb", [NA, GB, P], I32)
        weighted = sb("weighted", [P, GB, P])
        one_hot = sb("one_hot", [NA, GB, P], BF16)
        weighted_t = sb("weighted_t", [P, GB, P])
        nbr = sb("nbr", [P, GB, D])
        st_a = sb("st_a", [P, GB, 6])
        mv_a = sb("mv_a", [P, GB, 2])
        rs_a = sb("rs_a", [P, 2, GB])
        z_tok = sb("z_tok", [P, GB, D])
        en = sb("en", [P, 2, P])
        en1 = sb("en1", [P, 2, P])
        gz = sb("gz", [P, 2, P])
        hs = sb("hs", [P, 2, P])
        h_tok = sb("h_tok", [P, GB, D])
        st_b = sb("st_b", [P, GB, 6])
        mv_b = sb("mv_b", [P, GB, 2])
        rs_b = sb("rs_b", [P, 2, GB])
        y_tok = sb("y_tok", [P, GB, D])
        y_t = sb("y_t", [P, NP, P + HALF])
        g_sb = sb("g_sb", [P, H, NP, HALF])
        k_even = sb("k_even", [P, 2, 2, NP * HALF])
        qk_prod = sb("qk_prod", [P, 2, 2, NP * HALF])
        diag_s = sb("diag_s", [HALF, GB, H])
        v_odd = sb("v_odd", [P, GB, H // 2, 2, DH + 1])
        v_even = sb("v_even", [HALF, GB, H, DH])
        row_max = sb("row_max", [P, NP, 2 * H])
        probs = sb("probs", [P, NP, 2, H * HALF])
        p_diag = sb("p_diag", [HALF, NP, 2 * H])
        probs_t = sb("probs_t", [P, 2, 4, P])
        den = sb("den", [P, 2 * H])
        rden = sb("rden", [P, 2 * H])
        pdn = sb("pdn", [HALF, 2 * H])
        pv_even = sb("pv_even", [HALF, 2 * H, DH])
        zn = sb("zn", [P, 2 * H, DH])
        zt = sb("zt", [P, 2, 2, P])
        resid = sb("resid", [P, NB, D])
        st_c = sb("st_c", [P, GB, 6])
        mv_c = sb("mv_c", [P, GB, 2])
        rs_c = sb("rs_c", [P, 2, GB])
        rows = sb("rows", [P, 2, GB, ROW])
        y2 = sb("y2", [P, GB, D])
        y2_high = sb("y2_high", [P, GB, D])
        y2_t = sb("y2_t", [P, 2, P])
        lg = sb("lg", [P, GB, NE])
        lg2 = sb("lg2", [P, GB, NE])
        mx = sb("mx", [P, 2, GB])
        eq = sb("eq", [P, 2, GB, NE])
        rk = sb("rk", [P, 2, GB])
        oh = sb("oh", [P, 2, GB, NE])
        picked = sb("picked", [P, GB, NE], BF16)
        picked_before = sb("picked_before", [P, GB, NE], BF16)
        picked_all = sb("picked_all", [P, NE], BF16)
        slot = sb("slot", [P, GB, NE])
        slot2 = sb("slot2", [P, 2, GB, NE])
        slot_f = sb("slot_f", [P, 2, GB])
        slot_u = sb("slot_u", [P, 2, GB], U32)
        dmx = sb("dmx", [P, GB])
        ex = sb("ex", [P, GB])
        ex1 = sb("ex1", [P, GB])
        wt = sb("wt", [P, 2, GB])

        pads = sb("pads", [P, 2 * NE, ROW])
        tile_no = sb("tile_no", [P, 2])
        count = sb("count", [P, NE])
        tail_row = sb("tail_row", [P, NE], I32)
        cnt_r = sb("cnt_r", [P, NE], I32)
        cnt_m = sb("cnt_m", [P, NE], I32)
        n_tiles = sb("n_tiles", [P, NE])
        ones_e = sb("ones_e", [P, NE])
        tiles_to = sb("tiles_to", [P, NE])
        past = sb("past", [P, 2, NE])
        past_n = sb("past_n", [P, 2, NE])
        tile_e = sb("tile_e", [P, 2])
        tile_s = sb("tile_s", [P, 2])
        tile_d = sb("tile_d", [P, 2])
        tile_vals = sb("tile_vals", [P, 4])
        tile_table = sb("tile_table", [1, 2 * P + HALF], I32)
        x_rows = sb("x_rows", [P, QB, 4, ROW])
        x_t = sb("x_t", [P, 2, 4, P])
        silu = sb("silu", [P, 2, 4, P])
        hidden = sb("hidden", [P, 2, 4, P])
        hidden_t = sb("hidden_t", [P, 2, 4, P])
        y_rows = sb("y_rows", [P, QB, 4, D])
        NCH = 4
        CB = NB // NCH
        picked_out = [t[:, 0:NB * D].rearrange("p (b f) -> p b f", b=NB) for t in (ew12, ew12_high)]

        tail_ready, pads_written, table_ready, out_ready, stored, cnt_psum, table_psum, dve_route, added = (
            sem(n) for n in ("tail_ready", "pads_written", "table_ready", "out_ready", "stored", "cnt_psum",
                             "table_psum", "dve_route", "added"))
        x_loaded, rows_out = ([sem(f"{n}_q{q}") for q in range(QB)] for n in ("x_loaded", "rows_out"))
        xt_psum, xt_ready, up_psum, silu_ready, hid_ready, ht_psum, ht_ready, down_psum, o_ready = (
            [sem(f"{n}_{q}") for q in range(2)] for n in (
                "xt_psum", "xt_ready", "up_psum", "silu_ready", "hid_ready", "ht_psum", "ht_ready", "down_psum",
                "o_ready"))
        experts_loaded, high_ready, low_ready = sem("experts_loaded"), sem("high_ready"), sem("low_ready")
        consts_loaded, waits_passed = sem("consts_loaded"), sem("waits_passed")
        pool_const, dve_const, act_const, pe_const = (sem(n) for n in (
            "pool_const", "dve_const", "act_const", "pe_const"))
        pair_loaded, ids_loaded, adj_ready = sem("pair_loaded"), sem("ids_loaded"), sem("adj_ready")
        masked, onehot_ready, transposed_w, wt_ready, nb_psum, nb_ready, tok_psum = (sem(n) for n in (
            "masked", "onehot_ready", "transposed_w", "wt_ready", "nb_psum", "nb_ready", "tok_psum"))
        a_stats, a_rstd, b_stats, b_rstd, c_stats, c_rstd = (
            sem(n) for n in ("a_stats", "a_rstd", "b_stats", "b_rstd", "c_stats", "c_rstd"))
        a_norm, z_ready, z_psum, exp_ready, gz_ready, hs_ready, w2_psum, h_ready = (
            sem(n) for n in ("a_norm", "z_ready", "z_psum", "exp_ready", "gz_ready", "hs_ready", "w2_psum", "h_ready"))
        b_norm, y_ready, y_psum, yt_ready, resid_set = (sem(n) for n in (
            "b_norm", "y_ready", "y_psum", "yt_ready", "resid_set"))
        g_psum = [sem(f"g_psum{i}") for i in range(2)]
        g_ready = [sem(f"g_ready{i}") for i in range(2)]
        qk_psum = [sem(f"qk_psum{i}") for i in range(2)]
        ke_ready = [sem(f"ke_ready{i}") for i in range(2)]
        prod_ready = [sem(f"prod_ready{i}") for i in range(2)]
        diag_psum, diag_ready = sem("diag_psum"), sem("diag_ready")
        v_psum = [sem(f"v_psum{b}") for b in range(GB)]
        v_ready = [sem(f"v_ready{b}") for b in range(GB)]
        s_psum, max_step, sub_ready, dsub_ready, p_ready, pd_ready = (
            [sem(f"{n}{p}") for p in range(NP)] for n in (
                "s_psum", "max_step", "sub_ready", "dsub_ready", "p_ready", "pd_ready"))
        pt_psum = [sem(f"pt_psum{b}") for b in range(GB)]
        pt_ready = [sem(f"pt_ready{b}") for b in range(GB)]
        z_done = [sem(f"z_done{b}") for b in range(GB)]
        z_step, zn_ready, zt_psum, zt_ready, wo_psum, h2_ready = (
            [sem(f"{n}_{p}") for p in range(NP)] for n in (
                "z_step", "zn_ready", "zt_psum", "zt_ready", "wo_psum", "h2_ready"))
        y2_split = sem("y2_split")
        c_norm, y2_ready, y2_psum, y2t_ready, gate_psum, pick_step, gap_ready, ex_ready = (sem(n) for n in (
            "c_norm", "y2_ready", "y2_psum", "y2t_ready", "gate_psum", "pick_step", "gap_ready", "ex_ready"))
        picked_ready, before_chain, before_ready, rank_psum, slot_ready, slot_step = (
            sem(n) for n in ("picked_ready", "before_chain", "before_ready", "rank_psum", "slot_ready", "slot_step"))
        slotu_ready, w_step, w_put, rows_filled, dest_next, rows_sent = (sem(n) for n in (
            "slotu_ready", "w_step", "w_put", "rows_filled", "dest_next", "rows_sent"))

        def at_start(g, n):
            return isinstance(g, int) and g < n

        def at_end(g):
            return isinstance(g, int) and g == NG - 1

        def wait(eng, s, v):
            if isinstance(v, int) and v <= 0:
                return
            eng.wait_ge(s, v)

        def passed_by(eng):
            eng.sem_inc(waits_passed, 1)

        def ago(s, i, q, d):
            return s[(q - d) % 2], i * (QB // 2) + (q - d) // 2 + 1

        def bc(ap, n):
            return ap.unsqueeze(len(ap.shape)).broadcast_to([*ap.shape, n])

        block = ctx.enter_context(nc.Block())
        n_const = [0]
        DVE_CONSTS = 10
        pool_steps = [0]

        @block.sync
        def _(sp):
            def load(dst, src):
                sp.dma_start(dst, src).then_inc(consts_loaded, 16)
                n_const[0] += 16

            def row(ap):
                return ap.rearrange("(a n) -> a n", a=1)

            def col(ap):
                return ap.rearrange("(n a) -> n a", a=1)

            def group(g):
                wait(sp, masked, g)
                for par in range(2):
                    for dst, src in ((rel_sb, rel), (adj_sb, adj)):
                        sp.dma_start(
                            dst[par * HALF:(par + 1) * HALF, :, :],
                            src[bass.ds(g * GB, GB), par::2, :].rearrange("b t j -> t b j"),
                        ).then_inc(pair_loaded, 16)
                wait(sp, onehot_ready, g)
                sp.dma_start(ids_sb[:], ids[bass.ds(g * GB, GB), :].rearrange("b (a t) -> a b t", a=1)
                             .broadcast_to([NA, GB, P])).then_inc(ids_loaded, 16)

            sp.wait_ge(pool_const, 3)
            load(both_embed[:, 0:D], atom_embed)
            load(both_embed[:, D:2 * D], neighbor_embed)
            load(wrd_col[D:2 * D, :], col(w_rd))
            load(w1_bd[0:D, 0:D], w1[0:D, :])
            load(w1_bd[D:2 * D, D:2 * D], w1[D:2 * D, :])
            load(b1_bc[:], row(b1).broadcast_to([NA, D]))
            for i in range(2):
                load(film[i * D:(i + 1) * D, 0:1], col(gamma))
                load(film[i * D:(i + 1) * D, 1:2], col(beta))
                load(w2_bd[i * D:(i + 1) * D, i * D:(i + 1) * D], w2)
                load(gate_bd[i * D:(i + 1) * D, i * NE:(i + 1) * NE], gate_w)
            load(b2_bc[:], row(b2).broadcast_to([P, D]))
            for i, (w, b) in enumerate(((W_Q, b_Q), (W_K, b_K), (W_V, b_V))):
                load(qkv_raw[:, i, :].rearrange("m (h d) -> m h d", h=H), w.rearrange("h m d -> m h d"))
                for c in range(2):
                    load(bias_col[:, i, c:c + 1], col(b.rearrange("h d -> (h d)"))[c * P:(c + 1) * P, :])
            load(wo_sb[:], W_O.rearrange("(c h) d m -> (h d) c m", c=2))
            load(bo_bc[:], row(b_O).broadcast_to([P, D]))
            load(gateb_bc[:], row(gate_b).broadcast_to([P, NE]))
            group(0)
            for i, w in enumerate((ew1, ew2)):
                for half in range(2):
                    sp.dma_start(ew12[half * D:(half + 1) * D, :].rearrange("d (e i h) -> d i e h", e=NE, i=2)[:, i, :, :],
                                 w.rearrange("e d h -> d e h")).then_inc(experts_loaded, 16)
            sp.dma_start(ew3_sb[:].rearrange("h (e o) -> h e o", e=NE), ew3.rearrange("e h o -> h e o"))\
              .then_inc(experts_loaded, 16)
            sp.dma_start(sorted_rows[NE * REG:NE * REG + NE * P, :].rearrange("(i p) r -> p i r", p=P),
                         pads[:, NE:2 * NE, :]).then_inc(experts_loaded, 16)
            with sp.Fori(1, NG) as g:
                group(g)

            wait(sp, tail_ready, 1)
            for e in range(NE):
                r = sp.value_load(tail_row[0:1, e:e + 1], min_val=0, max_val=NE * REG - P)
                sp.dma_start(sorted_rows[bass.ds(r, P), :], pads[:, e, :]).then_inc(pads_written, 16)
            wait(sp, pads_written, 16 * NE)
            wait(sp, experts_loaded, 16 * 6)
            wait(sp, rows_sent, 128 * NG)
            wait(sp, table_ready, 1)

            def load_rows(i):
                for q in range(QB):
                    wait(sp, rows_out[q], i * 64)
                    for u in range(4):
                        r = sp.value_load(tile_table[0:1, bass.ds(i * (4 * QB) + 4 * q + u, 1)],
                                          min_val=0, max_val=NE * REG + (NE - 1) * P)
                        sp.dma_start(x_rows[:, q, u, :], sorted_rows[bass.ds(r, P), :]).then_inc(x_loaded[q], 16)

            load_rows(0)
            with sp.Fori(1, NQ // QB) as i:
                load_rows(i)

            for q in range(QB):
                wait(sp, rows_out[q], 64 * (NQ // QB))
            for c in range(NCH):
                for k in range(TOPK):
                    sp.dma_start(picked_out[k][:, c * CB:(c + 1) * CB, :],
                                 expert_out[k * NTOK:(k + 1) * NTOK, :].rearrange("(p b) f -> p b f", b=NB)[
                                     :, c * CB:(c + 1) * CB, :]).then_inc(x_loaded[c], 16)
            for c in range(NCH):
                wait(sp, out_ready, c + 1)
                for par in range(2):
                    sp.dma_start(out[c * CB:(c + 1) * CB, par::2, :].rearrange("b t f -> t b f"),
                                 resid[par * HALF:(par + 1) * HALF, c * CB:(c + 1) * CB, :]).then_inc(stored, 16)
            sp.wait_ge(stored, 32 * NCH)

        CONSTS = n_const[0]

        @block.gpsimd
        def _(pool):
            n = 0

            def step(ins):
                nonlocal n
                n += 1
                ins.then_inc(pool_const, 1)
                pool.wait_ge(pool_const, n)

            for t in (w1_bd, w2_bd, gate_bd, wrd_col):
                pool.memset(t[:], 0.0 if t is not wrd_col else 1.0)
            step(pool.memset(a_bd[:], 0.0))
            step(pool.memset(pads[:], 0.0))
            step(pool.iota(pads[:, :, ROW - 1:ROW].bitcast(I32), pattern=[[P, 2 * NE], [0, 1]], base=DUMP,
                           channel_multiplier=1))
            step(pool.memset(ident[:], 0.0))
            step(pool.affine_select(out=ident[:], in_=ident[:], compare_op=ALU.not_equal, fill=1.0, base=0,
                                    pattern=[[-1, P]], channel_multiplier=1))
            step(pool.memset(off_diag[:], 1.0))
            step(pool.affine_select(out=off_diag[:], in_=off_diag[:], compare_op=ALU.not_equal, fill=0.0,
                                    base=0, pattern=[[-1, P]], channel_multiplier=1))
            step(pool.tensor_copy(ident_b[:], ident[:]))
            step(pool.memset(causal[:], 0.0))
            step(pool.affine_select(out=causal[0:HALF, :].rearrange("p (h k) -> p h k", h=H),
                                    in_=causal[0:HALF, :].rearrange("p (h k) -> p h k", h=H),
                                    compare_op=ALU.is_gt, fill=-BIG, base=0,
                                    pattern=[[0, H], [-1, HALF]], channel_multiplier=1))
            step(pool.affine_select(out=causal[HALF:P, :].rearrange("p (h k) -> p h k", h=H),
                                    in_=causal[HALF:P, :].rearrange("p (h k) -> p h k", h=H),
                                    compare_op=ALU.is_ge, fill=-BIG, base=0,
                                    pattern=[[0, H], [-1, HALF]], channel_multiplier=1))
            step(pool.memset(eps_col[:], EPS))
            step(pool.memset(before[:], 1.0))
            step(pool.affine_select(out=before[:], in_=before[:], compare_op=ALU.is_gt, fill=0.0, base=0,
                                    pattern=[[1, P]], channel_multiplier=-1))
            step(pool.memset(ones_b[:], 1.0))
            step(pool.memset(head_sum[:], 1.0))
            for cmp_base, sign in ((0, 1), (DH - 1, -1)):
                step(pool.affine_select(out=head_sum[:], in_=head_sum[:], compare_op=ALU.is_ge, fill=0.0,
                                        base=cmp_base, pattern=[[-sign * DH, 4]], channel_multiplier=sign))
            step(pool.iota(tmp_i[:, 0:1], pattern=[[0, 1]], base=0, channel_multiplier=1))
            step(pool.tensor_copy(atom_no[:], tmp_i[:, 0:1]))
            step(pool.iota(tmp_i[:, 32:34], pattern=[[P, 2]], base=0, channel_multiplier=1))
            step(pool.tensor_copy(tile_no[:], tmp_i[:, 32:34]))
            step(pool.iota(tmp_i[:, 16:32], pattern=[[-1, NE]], base=NE, channel_multiplier=0))
            step(pool.tensor_copy(rev_e[:], tmp_i[:, 16:32]))
            step(pool.tensor_scalar(base_e[:], rev_e[:], -float(REG), float(NE * REG), ALU.mult, ALU.add))
            step(pool.iota(dest[:], pattern=[[NTOK, 2], [1, GB]], base=0, channel_multiplier=NB))
            step(pool.memset(y_tok[:, :, D - 1:D], 1.0))
            step(pool.memset(v_odd[:], 0.0))
            for par in range(2):
                step(pool.memset(v_odd[par * HALF:(par + 1) * HALF, :, :, par, DH:DH + 1], 1.0))
            step(pool.memset(picked_all[:], 0.0))
            step(pool.memset(quad_of[:], 0.0))
            for u in range(4):
                step(pool.affine_select(out=quad_of[:], in_=quad_of[:], compare_op=ALU.not_equal,
                                        fill=float(NE ** u), base=-u, pattern=[[-4, 32]], channel_multiplier=1))
            pool_steps[0] = n


            def mask(g):
                wait(pool, pair_loaded, (g + 1) * 64)
                wait(pool, transposed_w, g)
                passed_by(pool)
                pool.tensor_copy(adj_f[:], adj_sb[:]).then_inc(adj_ready, 1)
                pool.wait_ge(adj_ready, g + 1)
                pool.tensor_tensor(
                    weighted[:].rearrange("p b (two t) -> p b two t", two=2),
                    rel_sb[:].rearrange("p b (t two) -> p b two t", two=2),
                    adj_f[:].rearrange("p b (t two) -> p b two t", two=2), ALU.mult).then_inc(masked, 1)

            def one_hots(g):
                wait(pool, ids_loaded, (g + 1) * 16)
                wait(pool, nb_psum, g)
                passed_by(pool)
                pool.tensor_scalar(
                    one_hot[:].rearrange("p b (two t) -> p b two t", two=2),
                    ids_sb[:].rearrange("p b (t two) -> p b two t", two=2),
                    atom_no[0:NA, :], None, ALU.is_equal).then_inc(onehot_ready, 1)

            def set_resid(g):
                wait(pool, h_ready, g + 1)
                pool.tensor_tensor(resid[:, bass.ds(g * GB, GB), :], h_tok[:],
                                   bo_bc[:].unsqueeze(1).broadcast_to([P, GB, D]), ALU.add).then_inc(resid_set, 1)

            def route(g):
                wait(pool, picked_ready, g + 1)
                wait(pool, before_ready, g)
                passed_by(pool)
                pool.tensor_copy(picked_before[:, 0, :], picked_all[:]).then_inc(before_chain, 1)
                for b in range(1, GB):
                    wait(pool, before_chain, g * GB + b)
                    pool.tensor_tensor(picked_before[:, b, :], picked_before[:, b - 1, :], picked[:, b - 1, :],
                                       ALU.add).then_inc(before_chain, 1)
                wait(pool, before_chain, g * GB + GB)
                pool.tensor_tensor(picked_all[:], picked_before[:, GB - 1, :], picked[:, GB - 1, :],
                                   ALU.add).then_inc(before_ready, 1)

            def fill(g):
                wait(pool, y2_split, g + 1)
                wait(pool, rows_sent, g * 128)
                passed_by(pool)
                high = y2_high[:].unsqueeze(1).broadcast_to([P, 2, GB, D])
                pool.tensor_copy(rows[:, :, :, 0:D], high)
                pool.tensor_tensor(rows[:, :, :, D:2 * D], y2[:].unsqueeze(1).broadcast_to([P, 2, GB, D]), high,
                                   ALU.subtract)
                pool.tensor_copy(rows[:, :, :, ROW - 1:ROW].bitcast(U32),
                                 dest[:].unsqueeze(3)).then_inc(rows_filled, 1)
                pool.wait_ge(rows_filled, g + 1)
                passed_by(pool)
                pool.tensor_scalar(dest[:], dest[:], float(GB), None, ALU.add).then_inc(dest_next, 1)

            def send(g, first, last):
                if first == 0:
                    wait(pool, w_put, g + 1)
                    wait(pool, slotu_ready, g + 1)
                    wait(pool, dest_next, g + 1)
                    passed_by(pool)
                for i in range(first, last):
                    b, k = i // 2, i % 2
                    pool.indirect_dma_start(
                        sorted_rows, bass.IndirectOffsetOnAxis(ap=slot_u[:, k, b:b + 1], axis=0),
                        rows[:, k, b, :], None).then_inc(rows_sent, 16)

            mask(0)
            one_hots(0)
            set_resid(0)

            def body(g):
                if not at_end(g):
                    mask(g + 1)
                    one_hots(g + 1)
                if not at_start(g, 2):
                    send(g - 2, 0, 4)
                    send(g - 2, 4, 8)
                if not at_start(g, 1):
                    route(g - 1)
                if not at_end(g):
                    set_resid(g + 1)
                if not at_start(g, 1):
                    fill(g - 1)

            body(0)
            body(1)
            with pool.Fori(2, NG - 1) as g:
                body(g)
            body(NG - 1)
            send(NG - 2, 0, 8)
            route(NG - 1)
            fill(NG - 1)
            send(NG - 1, 0, 8)

            with pool.Fori(0, NQ // QB) as i:
                for q in range(QB):
                    wait(pool, *ago(o_ready, i, q, 0))
                    passed_by(pool)
                    for u in range(4):
                        pool.indirect_dma_start(
                            expert_out,
                            bass.IndirectOffsetOnAxis(ap=x_rows[:, q, u, ROW - 1:ROW].bitcast(U32), axis=0),
                            y_rows[:, q, u, :], None).then_inc(rows_out[q], 16)

        PC = pool_steps[0]

        @block.tensor
        def _(pe):
            n = 0

            def mm(out, lhsT, rhs, start=True, stop=True):
                return pe.matmul(out, lhsT, rhs, start=start, stop=stop, skip_group_check=True)

            pe.wait_ge(consts_loaded, CONSTS)
            pe.wait_ge(pool_const, PC)
            pe.transpose(ps_tok[:, 0:NA], both_embed[:], ident[0:NA, 0:NA]).then_inc(pe_const, 1)
            for i in range(3):
                for c in range(2):
                    last = pe.transpose(ps_pt[:, (i * 2 + c) * D:(i * 2 + c + 1) * D],
                                        qkv_raw[:, i, c * P:(c + 1) * P], ident[0:D, 0:D])
            last.then_inc(pe_const, 1)
            pe.wait_ge(dve_const, 1)
            mm(ps_g0[0:NA, 0:2 * D], embed_t[:], w1_bd[:]).then_inc(pe_const, 1)
            pe.wait_ge(dve_const, 2)
            for i in range(3):
                for c in range(2):
                    dst = (ps_tok if i < 2 else ps_g1)[:, (i % 2 * 2 + c) * P:(i % 2 * 2 + c + 1) * P]
                    last = pe.transpose(dst, qkv_t[:, i, c, :, :].rearrange("p a f -> p (a f)"), ident[:])
            last.then_inc(pe_const, 1)
            a_banks = [ps_scores[:, 0, :], ps_scores[:, 1, :], ps_z[:, 0, :], ps_z[:, 1, :]]
            for h in range(H):
                r, c = h % 4, h // 4
                at = slice(r * DH, (r + 1) * DH)
                last = mm(a_banks[r][:, c * D:(c + 1) * D],
                          qkv_t[at, 1, c, :, :].rearrange("p a f -> p (a f)"), qkv_t[at, 0, c, 0, :],
                          start=(c == 0))
            last.then_inc(pe_const, 1)

            def tok_weighted(g):
                wait(pe, masked, g + 1)
                wait(pe, v_ready[2], g)
                for b in range(GB):
                    last = pe.transpose(ps_g0[:, b * P:(b + 1) * P], weighted[:, b, :], ident[:])
                last.then_inc(transposed_w, 1)

            def tok_embed(g):
                wait(pe, onehot_ready, g + 1)
                wait(pe, h_ready, g)
                for b in range(GB):
                    for part in range(3):
                        last = mm(ps_tok[:, b * P:(b + 1) * P], one_hot[:, b, :], table_b[:, part, :],
                                  start=(b == 0 and part == 0))
                last.then_inc(nb_psum, 1)

            def tok_neighbors(g):
                wait(pe, wt_ready, g + 1)
                wait(pe, nb_ready, g + 1)
                for b in range(GB):
                    last = mm(ps_tok[:, b * P:b * P + D], weighted_t[:, b, :], nbr[:, b, :], start=False)
                last.then_inc(tok_psum, 1)

            def pair_transposes(dst, src):
                for p in range(NP):
                    last = pe.transpose(dst[:, p * P:(p + 1) * P],
                                        src[:, 2 * p:2 * p + 2, :].rearrange("p b f -> p (b f)"), ident[:])
                return last

            def tok_z(g):
                wait(pe, z_ready, g + 1)
                pair_transposes(ps_g0, z_tok).then_inc(z_psum, 1)

            def tok_w2(g):
                wait(pe, hs_ready, g + 1)
                for p in range(NP):
                    last = mm(ps_tok[:, p * P:(p + 1) * P], hs[:, p, :], w2_bd[:], start=(p == 0))
                last.then_inc(w2_psum, 1)

            def att_y(g):
                wait(pe, y_ready, g + 1)
                pair_transposes(ps_g0, y_tok).then_inc(y_psum, 1)

            def keys(g, i):
                wait(pe, yt_ready, g + 1)
                if i == 1:
                    wait(pe, v_ready[3], g)
                    wait(pe, slot_ready, g - 1)
                for h in range(4):
                    last = mm(ps_g[i][:, h * P:(h + 1) * P], a_bd[:, 4 * i + h, :], y_t[:, :, HALF:P],
                              start=(h == 0))
                last.then_inc(g_psum[i], 1)

            def even_qk(g, par):
                at = slice(par * D, (par + 1) * D)
                wait(pe, g_ready[par], g + 1)
                for i in range(2):
                    for c in range(2):
                        last = mm(ps_g[par][:, (2 * i + c) * P:(2 * i + c + 1) * P],
                                  qkv_w[at, i, c * P:(c + 1) * P], y_t[at, :, 0:HALF],
                                  start=(i + c == 0))
                last.then_inc(qk_psum[par], 1)

            def values(g, b):
                p, par = b // 2, b % 2
                at = slice(par * D, (par + 1) * D)
                if p == 0:
                    wait(pe, prod_ready[par], g + 1)
                else:
                    wait(pe, v_ready[par], g + 1)
                mm(ps_g[par][:, 0:2 * P], y_t[at, p, HALF:HALF + P], qkv_w[at, 2, :])
                mm(ps_g[par][0:HALF, 2 * P:4 * P], y_t[at, p, 0:HALF], qkv_w[at, 2, :],
                   start=False).then_inc(v_psum[b], 1)

            def diagonal(g):
                wait(pe, prod_ready[0], g + 1)
                wait(pe, prod_ready[1], g + 1)
                wait(pe, zt_ready[1], g)
                for par in range(2):
                    for p in range(NP):
                        for c in range(2):
                            col = (2 * p + par) * H + 4 * c
                            last = mm(ps_pt[0:HALF, col:col + 4], qk_prod[:, par, c, p * HALF:(p + 1) * HALF],
                                      head_sum[:], start=(par + p + c == 0))
                last.then_inc(diag_psum, 1)

            def scores(g, p):
                if p == 0:
                    wait(pe, sub_ready[1], g)
                    wait(pe, g_ready[0], g + 1)
                    wait(pe, g_ready[1], g + 1)
                else:
                    wait(pe, sub_ready[0], g + 1)
                for par in range(2):
                    at = slice(par * D, (par + 1) * D)
                    mm(ps_scores[:, par, :], ident_b[:], causal[:], stop=False)
                    last = mm(ps_scores[:, par, :], y_t[at, p, 0:P], g_sb[at, :, p, :], start=False)
                last.then_inc(s_psum[p], 1)

            def turn_probs(g, b):
                p, par = b // 2, b % 2
                wait(pe, p_ready[p], g + 1)
                wait(pe, (diag_ready, pt_ready[0], pt_ready[1], zt_ready[0])[b], g + 1)
                for j in range(4):
                    last = pe.transpose(ps_pt[:, j * P:(j + 1) * P], probs[:, p, par, j * P:(j + 1) * P], ident[:])
                last.then_inc(pt_psum[b], 1)

            def attend(g, b):
                par = b % 2
                wait(pe, pt_ready[b], g + 1)
                wait(pe, v_ready[b], g + 1)
                wait(pe, h2_ready[1 - b // 2], g + b // 2)
                w = 2 * (DH + 1)
                for j in range(4):
                    last = mm(ps_z[:, par, j * w:(j + 1) * w], probs_t[:, par, j, :],
                              v_odd[:, b, j, :, :], start=(j == 0))
                last.then_inc(z_done[b], 1)

            def turn_z(g, p):
                wait(pe, zn_ready[p], g + 1)
                wait(pe, pt_ready[2 + p], g + 1)
                for par in range(2):
                    for c in range(2):
                        last = pe.transpose(ps_pt[:, (2 * par + c) * P:(2 * par + c + 1) * P],
                                            zn[:, par * H + 4 * c:par * H + 4 * c + 4, :], ident[:])
                last.then_inc(zt_psum[p], 1)

            def project_out(g, p):
                wait(pe, zt_ready[p], g + 1)
                for par in range(2):
                    for c in range(2):
                        last = mm(ps_z[:, 0, 384 + par * D:384 + (par + 1) * D], zt[:, par, c, :], wo_sb[:, c, :],
                                  start=(par + c == 0))
                last.then_inc(wo_psum[p], 1)

            def gate_y(g):
                wait(pe, y2_ready, g + 1)
                wait(pe, v_ready[3], NG if at_end(g) else g + 2)
                pair_transposes(ps_g1, y2).then_inc(y2_psum, 1)

            def gate(g):
                wait(pe, y2t_ready, g + 1)
                for p in range(NP):
                    last = mm(ps_g1[:, 256 + 2 * NE * p:256 + 2 * NE * (p + 1)], y2_t[:, p, :], gate_bd[:],
                              start=(p == 0))
                last.then_inc(gate_psum, 1)

            def rank(g):
                wait(pe, picked_ready, g + 1)
                wait(pe, before_ready, g + 1)
                mm(ps_g1[:, 384:384 + GB * NE], before[:], picked[:].rearrange("p b e -> p (b e)"))
                mm(ps_g1[:, 384:384 + GB * NE], ones_b[:], picked_before[:].rearrange("p b e -> p (b e)"),
                   start=False).then_inc(rank_psum, 1)

            pe.wait_ge(dve_const, DVE_CONSTS)
            pe.wait_ge(act_const, 1)
            tok_weighted(0)
            tok_embed(0)
            tok_neighbors(0)
            tok_z(0)
            tok_w2(0)
            att_y(0)
            keys(0, 0)
            keys(0, 1)
            even_qk(0, 0)
            even_qk(0, 1)
            values(0, 0)
            values(0, 1)
            values(0, 2)
            values(0, 3)
            diagonal(0)

            def body(g):
                scores(g, 0)
                if not at_end(g):
                    tok_weighted(g + 1)
                    tok_embed(g + 1)
                if not at_start(g, 1):
                    gate_y(g - 1)
                scores(g, 1)
                if not at_end(g):
                    tok_neighbors(g + 1)
                if not at_start(g, 1):
                    gate(g - 1)
                turn_probs(g, 0)
                if not at_end(g):
                    tok_z(g + 1)
                turn_probs(g, 1)
                attend(g, 0)
                attend(g, 1)
                if not at_start(g, 1):
                    rank(g - 1)
                turn_probs(g, 2)
                if not at_end(g):
                    tok_w2(g + 1)
                turn_z(g, 0)
                turn_probs(g, 3)
                project_out(g, 0)
                if not at_end(g):
                    att_y(g + 1)
                attend(g, 2)
                attend(g, 3)
                if not at_end(g):
                    keys(g + 1, 0)
                    keys(g + 1, 1)
                    even_qk(g + 1, 0)
                    even_qk(g + 1, 1)
                turn_z(g, 1)
                if not at_end(g):
                    values(g + 1, 0)
                    values(g + 1, 1)
                project_out(g, 1)
                if not at_end(g):
                    values(g + 1, 2)
                    values(g + 1, 3)
                    diagonal(g + 1)

            body(0)
            with pe.Fori(1, NG - 1) as g:
                body(g)
            body(NG - 1)
            g = NG - 1
            gate_y(g)
            gate(g)
            rank(g)

            wait(pe, slot_ready, NG)
            mm(ps_tok[:, 0:NE], ones_b[:], picked_all[:]).then_inc(cnt_psum, 1)
            wait(pe, dve_route, 1)
            for j in range(2):
                mm(ps_pt[0:1, j * P:(j + 1) * P], tile_vals[:, j:j + 1], ident[:], start=(j == 0))
                last = mm(ps_pt[0:1, 2 * P + j * 32:2 * P + (j + 1) * 32], tile_vals[:, 2 + j:3 + j], quad_of[:],
                          start=False)
            last.then_inc(table_psum, 1)
            wait(pe, table_ready, 1)
            wait(pe, high_ready, 2 * NG)
            wait(pe, low_ready, NG)

            def experts_of(at):
                packed = pe.value_load(tile_table[0:1, bass.ds(at + 2 * P, 1)], min_val=0, max_val=NE ** 4 - 1)
                return [(packed >> (4 * u)) & (NE - 1) for u in range(4)]

            def turn(i, q):
                wait(pe, x_loaded[q], (i + 1) * 64)
                wait(pe, *ago(xt_ready, i, q, 1))
                passed_by(pe)
                for u in range(4):
                    last = pe.transpose(ps_g0[:, u * P:(u + 1) * P], x_rows[:, q, u, 0:2 * D], ident[:])
                last.then_inc(xt_psum[q % 2], 1)

            def up(i, q, experts):
                wait(pe, *ago(xt_ready, i, q, 0))
                wait(pe, *ago(hid_ready, i, q, 2))
                passed_by(pe)
                bank = (ps_scores, ps_z)[q % 2]
                for u, e in enumerate(experts):
                    for part in (ew12_high, ew12):
                        last = mm(bank[:, u // 2, u % 2 * 2 * HID:(u % 2 + 1) * 2 * HID],
                                  x_t[:, q % 2, u, :].bitcast(F32R),
                                  part[:, bass.ds(e * (2 * HID), 2 * HID)].bitcast(F32R),
                                  start=(u % 2 == 0 and part is ew12_high))
                last.then_inc(up_psum[q % 2], 1)

            def turn_hidden(i, q):
                wait(pe, *ago(hid_ready, i, q, 0))
                wait(pe, *ago(ht_ready, i, q, 1))
                for u in range(4):
                    last = pe.transpose(ps_g1[:, u * P:(u + 1) * P], hidden[:, q % 2, u, :], ident[:])
                last.then_inc(ht_psum[q % 2], 1)

            def down(i, q, experts):
                wait(pe, *ago(ht_ready, i, q, 0))
                wait(pe, *ago(o_ready, i, q, 2))
                passed_by(pe)
                for u, e in enumerate(experts):
                    last = mm((ps_tok, ps_pt)[q % 2][:, u * D:(u + 1) * D], hidden_t[:, q % 2, u, :],
                              ew3_sb[:, bass.ds(e * D, D)], start=(u == 0))
                last.then_inc(down_psum[q % 2], 1)

            def at(i, q):
                return (i, q) if q >= 0 else (i - 1, q + QB)

            def round_(i, first=False, last=False):
                experts = {q: experts_of(i * QB + q) for q in ((-2, -1) if not first else ())}
                for q in range(QB):
                    experts[q] = experts_of(i * QB + q)
                    if q + 1 < QB:
                        turn(i, q + 1)
                    elif not last:
                        turn(i + 1, 0)
                    if q >= 2 or not first:
                        down(*at(i, q - 2), experts[q - 2])
                    up(i, q, experts[q])
                    if q >= 1 or not first:
                        turn_hidden(*at(i, q - 1))
                return experts

            N = NQ // QB
            turn(0, 0)
            round_(0, first=True)
            with pe.Fori(1, N - 1) as i:
                round_(i)
            experts = round_(N - 1, last=True)
            down(N - 1, QB - 2, experts[QB - 2])
            turn_hidden(N - 1, QB - 1)
            down(N - 1, QB - 1, experts[QB - 1])

        @block.scalar
        def _(act):
            act.add_instruction(mybir.InstLoadActFuncSet(
                name=nc.get_next_instruction_name(), engine=act.engine, act_func_set_id=EXP_LN_SET))
            act.wait_ge(pe_const, 5)
            act.wait_ge(pool_const, PC)
            for r in range(4):
                bank = (ps_scores if r < 2 else ps_z)[:, r % 2, 0:2 * D]
                for i in range(2):
                    at = slice(i * D, (i + 1) * D)
                    last = act.activation(a_bd[at, r::4, i * D:(i + 1) * D],
                                          bank[at, :].rearrange("p (c f) -> p c f", c=2), ACT.Copy)
            last.then_inc(act_const, 1)
            act.wait_ge(dve_const, DVE_CONSTS)

            def tok_nbr(g):
                wait(act, nb_psum, g + 1)
                wait(act, tok_psum, g)
                act.activation(nbr[:], ps_tok[:].rearrange("p (b f) -> p b f", b=GB)[:, :, D:2 * D],
                               ACT.Copy).then_inc(nb_ready, 1)

            def rstd(g, mv, rs, stats, ready):
                wait(act, stats, g + 1)
                act.activation(rs[:, 0, :], mv[:, :, 1], ACT.Ln, bias=eps_col[:]).then_inc(ready, 1)
                wait(act, ready, g * 2 + 1)
                act.activation(rs[:, 1, :], rs[:, 0, :], ACT.Exp, scale=-0.5).then_inc(ready, 1)

            def tok_exp(g):
                wait(act, z_psum, g + 1)
                wait(act, hs_ready, g)
                act.activation(en[:].rearrange("p c t -> p (c t)"), ps_g0[:, 0:2 * P], ACT.Exp,
                               scale=film[:, 2:3], bias=film[:, 3:4]).then_inc(exp_ready, 1)

            def att_yt(g):
                wait(act, y_psum, g + 1)
                wait(act, s_psum[1], g)
                src = ps_g0[:, 0:2 * P].rearrange("p (c t) -> p c t", c=NP)
                act.activation(y_t[:, :, 0:P], src, ACT.Copy)
                act.activation(y_t[:, :, P:P + HALF], src[:, :, HALF:P], ACT.Copy).then_inc(yt_ready, 1)

            def keys(g, i):
                wait(act, g_psum[i], g + 1)
                act.activation(g_sb[:, 4 * i:4 * i + 4, :, :].rearrange("p h c k -> p (h c k)"),
                               ps_g[i][:], ACT.Copy).then_inc(g_ready[i], 1)

            def even_k(g, par):
                wait(act, qk_psum[par], g + 1)
                wait(act, prod_ready[par], g)
                act.activation(k_even[:, par, :, :].rearrange("p c t -> p (c t)"),
                               ps_g[par][:, 2 * P:4 * P], ACT.Copy).then_inc(ke_ready[par], 1)

            def values(g, b):
                par = b % 2
                wait(act, v_psum[b], g + 1)
                wait(act, z_done[b], g)
                for i in range(2):
                    at = slice(i * HALF, (i + 1) * HALF)
                    act.activation(v_odd[at, b, :, i, 0:DH],
                                   ps_g[par][at, 0:2 * P].rearrange("p (j i d) -> p j i d", i=2, d=DH)[:, :, i, :],
                                   ACT.Copy)
                wait(act, zn_ready[b // 2], g)
                act.activation(v_even[:, b, :, :].rearrange("p h d -> p (h d)"),
                               ps_g[par][0:HALF, 2 * P:4 * P], ACT.Copy).then_inc(v_ready[b], 1)

            def softmax(g, p):
                wait(act, sub_ready[p], g + 1)
                q = probs[:, p, :, :].rearrange("p c k -> p (c k)")
                act.activation(q, q, ACT.Exp).then_inc(p_ready[p], 1)
                wait(act, dsub_ready[p], g + 1)
                act.activation(p_diag[:, p, :], p_diag[:, p, :], ACT.Exp).then_inc(pd_ready[p], 1)

            def turn_probs(g, b):
                wait(act, pt_psum[b], g + 1)
                wait(act, z_done[(b + 2) % 4], g + b // 2)
                act.activation(probs_t[:, b % 2, :, :].rearrange("p j t -> p (j t)"), ps_pt[:], ACT.Copy)\
                   .then_inc(pt_ready[b], 1)

            def turn_z(g, p):
                wait(act, zt_psum[p], g + 1)
                wait(act, wo_psum[1 - p], g + p)
                act.activation(zt[:].rearrange("p b c t -> p (b c t)"), ps_pt[:], ACT.Copy).then_inc(zt_ready[p], 1)

            def gate_y(g):
                wait(act, y2_psum, g + 1)
                act.activation(y2_t[:].rearrange("p c t -> p (c t)"), ps_g1[:, 0:2 * P], ACT.Copy)\
                   .then_inc(y2t_ready, 1)

            def gap(g):
                wait(act, gap_ready, g + 1)
                act.activation(ex[:], dmx[:], ACT.Exp).then_inc(ex_ready, 1)

            tok_nbr(0)
            rstd(0, mv_a, rs_a, a_stats, a_rstd)
            tok_exp(0)
            rstd(0, mv_b, rs_b, b_stats, b_rstd)
            att_yt(0)
            keys(0, 0)
            keys(0, 1)
            even_k(0, 0)
            even_k(0, 1)
            values(0, 0)
            values(0, 1)
            values(0, 2)
            values(0, 3)

            def body(g):
                if not at_end(g):
                    tok_nbr(g + 1)
                if not at_start(g, 1):
                    rstd(g - 1, mv_c, rs_c, c_stats, c_rstd)
                softmax(g, 0)
                if not at_end(g):
                    rstd(g + 1, mv_a, rs_a, a_stats, a_rstd)
                if not at_start(g, 1):
                    gate_y(g - 1)
                softmax(g, 1)
                turn_probs(g, 0)
                if not at_end(g):
                    tok_exp(g + 1)
                turn_probs(g, 1)
                if not at_start(g, 1):
                    gap(g - 1)
                turn_probs(g, 2)
                turn_z(g, 0)
                if not at_end(g):
                    rstd(g + 1, mv_b, rs_b, b_stats, b_rstd)
                    att_yt(g + 1)
                turn_probs(g, 3)
                if not at_end(g):
                    keys(g + 1, 0)
                    keys(g + 1, 1)
                    even_k(g + 1, 0)
                    even_k(g + 1, 1)
                turn_z(g, 1)
                if not at_end(g):
                    values(g + 1, 0)
                    values(g + 1, 1)
                    values(g + 1, 2)
                    values(g + 1, 3)

            body(0)
            with act.Fori(1, NG - 1) as g:
                body(g)
            body(NG - 1)
            g = NG - 1
            rstd(g, mv_c, rs_c, c_stats, c_rstd)
            gate_y(g)
            gap(g)

            def turned(i, q):
                wait(act, *ago(xt_psum, i, q, 0))
                wait(act, *ago(up_psum, i, q, 2))
                act.activation(x_t[:, q % 2, :, :].rearrange("p u t -> p (u t)").bitcast(F32R), ps_g0[:], ACT.Copy)\
                   .then_inc(xt_ready[q % 2], 1)

            def turned_hidden(i, q):
                wait(act, *ago(ht_psum, i, q, 0))
                wait(act, *ago(down_psum, i, q, 2))
                act.activation(hidden_t[:, q % 2, :, :].rearrange("p u t -> p (u t)"), ps_g1[:], ACT.Copy)\
                   .then_inc(ht_ready[q % 2], 1)

            def gated(i, q):
                wait(act, *ago(up_psum, i, q, 0))
                wait(act, *ago(hid_ready, i, q, 2))
                h1 = (ps_scores, ps_z)[q % 2][:].rearrange("p c (u i h) -> p (c u) i h", u=2, i=2)[:, :, 0, :]
                act.activation(silu[:, q % 2, :, :], h1, ACT.Silu).then_inc(silu_ready[q % 2], 1)

            def round_(i, first=False, last=False):
                for q in range(QB):
                    if q + 1 < QB:
                        turned(i, q + 1)
                    elif not last:
                        turned(i + 1, 0)
                    gated(i, q)
                    if q:
                        turned_hidden(i, q - 1)
                    elif not first:
                        turned_hidden(i - 1, QB - 1)

            N = NQ // QB
            turned(0, 0)
            round_(0, first=True)
            with act.Fori(1, N - 1) as i:
                round_(i)
            round_(N - 1, last=True)
            turned_hidden(N - 1, QB - 1)

        @block.vector
        def _(dve):
            n = 0

            def step(ins):
                nonlocal n
                n += 1
                ins.then_inc(dve_const, 1)
                dve.wait_ge(dve_const, n)

            dve.wait_ge(consts_loaded, CONSTS)
            dve.wait_ge(pool_const, PC)
            dve.wait_ge(pe_const, 1)
            step(dve.tensor_scalar(embed_t[:], ps_tok[:, 0:NA], wrd_col[:], None, ALU.mult))
            dve.wait_ge(pe_const, 2)
            for i in range(3):
                s = SCALE if i == 0 else 1.0
                for c in range(2):
                    src = ps_pt[:, (i * 2 + c) * D:(i * 2 + c + 1) * D]
                    for a in range(2):
                        dve.tensor_scalar(qkv_t[:, i, c, a, 0:D - 1], src[:, 0:D - 1], src[:, D - 1:D], s,
                                          ALU.subtract, ALU.mult)
                        ins = dve.tensor_scalar(qkv_t[:, i, c, a, D - 1:D], bias_col[:, i, c:c + 1], s, None,
                                                ALU.mult)
            step(ins)
            dve.wait_ge(pe_const, 3)
            dve.tensor_copy(table[:, D:2 * D], ps_g0[0:NA, D:2 * D])
            step(dve.tensor_tensor(table[:, 0:D], ps_g0[0:NA, 0:D], b1_bc[:], ALU.add))
            step(dve.tensor_copy(table_b[:, 0, :], table[:]))
            step(dve.tensor_tensor(table_r[:], table[:], table_b[:, 0, :], ALU.subtract))
            step(dve.tensor_copy(table_b[:, 1, :], table_r[:]))
            step(dve.tensor_tensor(table[:], table_r[:], table_b[:, 1, :], ALU.subtract))
            step(dve.tensor_copy(table_b[:, 2, :], table[:]))
            step(dve.tensor_scalar(film[:, 2:4], film[:, 0:2], -1.0, None, ALU.mult))
            dve.wait_ge(pe_const, 4)
            for i in range(3):
                src = (ps_tok if i < 2 else ps_g1)[:, i % 2 * 2 * P:(i % 2 + 1) * 2 * P]
                ins = dve.tensor_copy(qkv_w[:, i, :], src)
            step(ins)
            assert n == DVE_CONSTS


            def stats_of(g, src, st, mv, sems):
                chain, stats, rstd, ready = sems
                for b in range(GB):
                    ins = dve.bn_stats(st[:, b, :], src(b))
                ins.then_inc(chain, 1)
                dve.wait_ge(chain, g + 1)
                passed_by(dve)
                for b in range(GB):
                    ins = dve.bn_aggr(mv[:, b, :], st[:, b, :])
                ins.then_inc(stats, 1)

            def norm(g, src, mv, rs, dst, width, sems):
                chain, stats, rstd, ready = sems
                wait(dve, rstd, g * 2 + 2)
                for b in range(GB):
                    ins = dve.tensor_scalar(dst[:, b, 0:width], src(b)[:, 0:width], mv[:, b, 0:1], rs[:, 1, b:b + 1],
                                            ALU.subtract, ALU.mult)
                ins.then_inc(ready, 1)

            def tok_wt(g):
                wait(dve, transposed_w, g + 1)
                wait(dve, tok_psum, g)
                dve.tensor_tensor(weighted_t[:], ps_g0[:].rearrange("p (b t) -> p b t", b=GB),
                                  off_diag[:].unsqueeze(1).broadcast_to([P, GB, P]), ALU.mult).then_inc(wt_ready, 1)

            sems_a = (a_norm, a_stats, a_rstd, z_ready)
            sems_b = (b_norm, b_stats, b_rstd, y_ready)
            sems_c = (c_norm, c_stats, c_rstd, y2_ready)

            def tok_stats(g):
                wait(dve, tok_psum, g + 1)
                stats_of(g, lambda b: ps_tok[:, b * P:b * P + D], st_a, mv_a, sems_a)

            def tok_norm(g):
                wait(dve, z_psum, g)
                norm(g, lambda b: ps_tok[:, b * P:b * P + D], mv_a, rs_a, z_tok, D, sems_a)

            def tok_silu(g):
                wait(dve, exp_ready, g + 1)
                dve.tensor_scalar(gz[:].rearrange("p c t -> p (c t)"), ps_g0[:, 0:2 * P], film[:, 0:1], film[:, 1:2],
                                  ALU.mult, ALU.add).then_inc(gz_ready, 1)
                dve.tensor_scalar(en1[:], en[:], 1.0, None, ALU.add).then_inc(gz_ready, 1)
                dve.wait_ge(gz_ready, g * 3 + 2)
                dve.reciprocal(en1[:], en1[:]).then_inc(gz_ready, 1)
                dve.wait_ge(gz_ready, g * 3 + 3)
                wait(dve, w2_psum, g)
                dve.tensor_tensor(hs[:], en1[:], gz[:], ALU.mult).then_inc(hs_ready, 1)

            def tok_h(g):
                wait(dve, w2_psum, g + 1)
                wait(dve, resid_set, g)
                dve.tensor_tensor(h_tok[:], ps_tok[:, 0:GB * D].rearrange("p (b f) -> p b f", b=GB),
                                  b2_bc[:].unsqueeze(1).broadcast_to([P, GB, D]), ALU.add).then_inc(h_ready, 1)
                dve.wait_ge(h_ready, g + 1)
                passed_by(dve)
                stats_of(g, lambda b: h_tok[:, b, :], st_b, mv_b, sems_b)

            def y_norm(g):
                wait(dve, y_psum, g)
                norm(g, lambda b: h_tok[:, b, :], mv_b, rs_b, y_tok, D - 1, sems_b)

            def products(g, par):
                wait(dve, ke_ready[par], g + 1)
                wait(dve, diag_psum, g)
                dve.tensor_tensor(qk_prod[:, par, :, :].rearrange("p c t -> p (c t)"), ps_g[par][:, 0:2 * P],
                                  k_even[:, par, :, :].rearrange("p c t -> p (c t)"),
                                  ALU.mult).then_inc(prod_ready[par], 1)

            def diagonal(g):
                wait(dve, diag_psum, g + 1)
                wait(dve, dsub_ready[1], g)
                dve.tensor_copy(diag_s[:].rearrange("p b h -> p (b h)"), ps_pt[0:HALF, 0:GB * H])\
                   .then_inc(diag_ready, 1)

            def softmax(g, p):
                wait(dve, s_psum[p], g + 1)
                s = ps_scores[:].rearrange("p c (h k) -> p (c h) k", h=H)
                d = diag_s[:, 2 * p:2 * p + 2, :].rearrange("p b h -> p (b h)")
                dve.tensor_reduce(row_max[:, p, :], s, AXX, ALU.max).then_inc(max_step[p], 1)
                dve.wait_ge(max_step[p], g * 2 + 1)
                dve.wait_ge(diag_ready, g + 1)
                dve.tensor_tensor(row_max[0:HALF, p, :], row_max[0:HALF, p, :], d, ALU.max).then_inc(max_step[p], 1)
                dve.wait_ge(max_step[p], g * 2 + 2)
                wait(dve, pt_psum[2 * p + 1], g)
                dve.tensor_tensor(probs[:, p, :, :].rearrange("p c (h k) -> p (c h) k", h=H), s,
                                  bc(row_max[:, p, :], HALF), ALU.subtract).then_inc(sub_ready[p], 1)
                dve.tensor_tensor(p_diag[:, p, :], d, row_max[0:HALF, p, :], ALU.subtract).then_inc(dsub_ready[p], 1)

            def normalize(g, p):
                wait(dve, z_done[2 * p + 1], g + 1)
                w = DH + 1
                z = ps_z[:, :, 0:H * w].rearrange("p c (h w) -> p c h w", w=w)
                den_v = den[:].rearrange("p (c h) -> p c h", c=2)
                dve.tensor_copy(den_v, z[:, :, :, DH]).then_inc(z_step[p], 1)
                dve.wait_ge(z_step[p], g * 6 + 1)
                dve.wait_ge(pd_ready[p], g + 1)
                dve.tensor_tensor(den[0:HALF, :], den[0:HALF, :], p_diag[:, p, :], ALU.add).then_inc(z_step[p], 1)
                dve.wait_ge(z_step[p], g * 6 + 2)
                dve.reciprocal(rden[:], den[:]).then_inc(z_step[p], 1)
                dve.wait_ge(z_step[p], g * 6 + 3)
                dve.tensor_tensor(pdn[:], p_diag[:, p, :], rden[0:HALF, :], ALU.mult).then_inc(z_step[p], 1)
                if p == 0:
                    wait(dve, zt_psum[1], g)
                else:
                    wait(dve, zt_psum[0], g + 1)
                dve.tensor_tensor(zn[:].rearrange("p (c h) d -> p c h d", c=2), z[:, :, :, 0:DH],
                                  bc(rden[:].rearrange("p (c h) -> p c h", c=2), DH), ALU.mult).then_inc(z_step[p], 1)
                dve.wait_ge(z_step[p], g * 6 + 4)
                dve.tensor_tensor(pv_even[:], v_even[:, 2 * p:2 * p + 2, :, :].rearrange("p b h d -> p (b h) d"),
                                  bc(pdn[:], DH), ALU.mult).then_inc(z_step[p], 1)
                dve.wait_ge(z_step[p], g * 6 + 6)
                dve.wait_ge(z_step[p], g * 6 + 5)
                dve.tensor_tensor(zn[0:HALF, :, :], zn[0:HALF, :, :], pv_even[:], ALU.add).then_inc(zn_ready[p], 1)

            def add_attention(g, p):
                wait(dve, wo_psum[p], g + 1)
                wait(dve, resid_set, g + 1)
                r = resid[:, bass.ds(g * GB + 2 * p, 2), :]
                dve.tensor_tensor(r, ps_z[:, 0, 384:384 + 2 * D].rearrange("p (b f) -> p b f", b=2), r,
                                  ALU.add).then_inc(h2_ready[p], 1)

            def pick(g, k, src, at):
                dve.tensor_reduce(mx[:, k, :], src, AXX, ALU.max).then_inc(pick_step, 1)
                dve.wait_ge(pick_step, g * 12 + at + 1)
                dve.tensor_tensor(eq[:, k, :, :], src, bc(mx[:, k, :], NE), ALU.is_equal).then_inc(pick_step, 1)
                dve.wait_ge(pick_step, g * 12 + at + 2)
                rev = rev_e[:].unsqueeze(1).broadcast_to([P, GB, NE])
                dve.tensor_tensor(eq[:, k, :, :], eq[:, k, :, :], rev, ALU.mult).then_inc(pick_step, 1)
                dve.wait_ge(pick_step, g * 12 + at + 3)
                dve.tensor_reduce(rk[:, k, :], eq[:, k, :, :], AXX, ALU.max).then_inc(pick_step, 1)
                dve.wait_ge(pick_step, g * 12 + at + 4)
                dve.tensor_tensor(oh[:, k, :, :], rev, bc(rk[:, k, :], NE), ALU.is_equal).then_inc(pick_step, 1)
                dve.wait_ge(pick_step, g * 12 + at + 5)

            def resid_of(g):
                return lambda b: resid[:, bass.ds(g * GB + b, 1), :].rearrange("p b f -> p (b f)")

            def gate_stats(g):
                dve.wait_ge(h2_ready[1], g + 1)
                passed_by(dve)
                stats_of(g, resid_of(g), st_c, mv_c, sems_c)

            def gate_norm(g):
                wait(dve, rows_filled, g)
                norm(g, resid_of(g), mv_c, rs_c, y2, D, sems_c)

            def gate_split(g):
                dve.wait_ge(y2_ready, g + 1)
                dve.tensor_scalar(y2_high[:].bitcast(U32), y2[:].bitcast(U32), HIGH_BITS, None, ALU.bitwise_and)\
                   .then_inc(y2_split, 1)

            def split_weights(g):
                wait(dve, experts_loaded, 16 * 6)
                at = bass.ds(g * WS, WS)
                wait(dve, low_ready, g)
                dve.tensor_scalar(high_u[:], ew12[:, at].bitcast(U32), HIGH_BITS, None, ALU.bitwise_and)\
                   .then_inc(high_ready, 1)
                dve.wait_ge(high_ready, g * 2 + 1)
                dve.tensor_copy(ew12_high[:, at].bitcast(F32R), high_u[:].bitcast(F32)).then_inc(high_ready, 1)
                dve.tensor_tensor(ew12[:, at].bitcast(F32R), ew12[:, at], high_u[:].bitcast(F32), ALU.subtract)\
                   .then_inc(low_ready, 1)

            def gate(g):
                wait(dve, gate_psum, g + 1)
                dve.tensor_tensor(lg[:], ps_g1[:, 256:256 + GB * NE].rearrange("p (b e) -> p b e", b=GB),
                                  gateb_bc[:].unsqueeze(1).broadcast_to([P, GB, NE]), ALU.add).then_inc(pick_step, 1)
                dve.wait_ge(pick_step, g * 12 + 1)
                pick(g, 0, lg[:], 1)
                dve.scalar_tensor_tensor(lg2[:], oh[:, 0, :, :], -3.0e38, lg[:], ALU.mult, ALU.add)\
                   .then_inc(pick_step, 1)
                dve.wait_ge(pick_step, g * 12 + 7)
                pick(g, 1, lg2[:], 7)
                wait(dve, rank_psum, g)
                dve.tensor_tensor(picked[:], oh[:, 0, :, :], oh[:, 1, :, :], ALU.add).then_inc(picked_ready, 1)
                dve.tensor_tensor(dmx[:], mx[:, 1, :], mx[:, 0, :], ALU.subtract).then_inc(gap_ready, 1)

            def weigh_picks(g):
                wait(dve, ex_ready, g + 1)
                dve.tensor_scalar(ex1[:], ex[:], 1.0, None, ALU.add).then_inc(w_step, 1)
                dve.wait_ge(w_step, g * 3 + 1)
                dve.reciprocal(wt[:, 0, :], ex1[:]).then_inc(w_step, 1)
                dve.wait_ge(w_step, g * 3 + 2)
                dve.tensor_tensor(wt[:, 1, :], wt[:, 0, :], ex[:], ALU.mult).then_inc(w_step, 1)
                dve.wait_ge(w_step, g * 3 + 3)
                wait(dve, rows_sent, g * 128)
                dve.tensor_copy(rows[:, :, :, 2 * D], wt[:]).then_inc(w_put, 1)

            def slots(g):
                wait(dve, rank_psum, g + 1)
                dve.tensor_tensor(slot[:], ps_g1[:, 384:384 + GB * NE].rearrange("p (b e) -> p b e", b=GB),
                                  base_e[:].unsqueeze(1).broadcast_to([P, GB, NE]), ALU.add).then_inc(slot_ready, 1)
                dve.wait_ge(slot_ready, g + 1)
                dve.tensor_tensor(slot2[:], oh[:], slot[:].unsqueeze(1).broadcast_to([P, 2, GB, NE]), ALU.mult)\
                   .then_inc(slot_step, 1)
                dve.wait_ge(slot_step, g * 2 + 1)
                dve.tensor_reduce(slot_f[:], slot2[:], AXX, ALU.add).then_inc(slot_step, 1)
                dve.wait_ge(slot_step, g * 2 + 2)
                dve.tensor_copy(slot_u[:], slot_f[:]).then_inc(slotu_ready, 1)

            tok_wt(0)
            tok_stats(0)
            tok_norm(0)
            tok_silu(0)
            tok_h(0)
            y_norm(0)
            products(0, 1)
            products(0, 0)
            diagonal(0)

            def body(g):
                if not at_start(g, 1):
                    gate_stats(g - 1)
                softmax(g, 0)
                if not at_start(g, 1):
                    gate_norm(g - 1)
                    gate_split(g - 1)
                if not at_end(g):
                    tok_wt(g + 1)
                softmax(g, 1)
                if not at_end(g):
                    tok_stats(g + 1)
                    tok_norm(g + 1)
                if not at_start(g, 1):
                    gate(g - 1)
                if not at_end(g):
                    tok_silu(g + 1)
                if not at_start(g, 1):
                    weigh_picks(g - 1)
                normalize(g, 0)
                if not at_end(g):
                    tok_h(g + 1)
                    y_norm(g + 1)
                split_weights(g)
                add_attention(g, 0)
                if not at_start(g, 1):
                    slots(g - 1)
                normalize(g, 1)
                if not at_end(g):
                    products(g + 1, 1)
                    products(g + 1, 0)
                    diagonal(g + 1)
                add_attention(g, 1)

            body(0)
            with dve.Fori(1, NG - 1) as g:
                body(g)
            body(NG - 1)
            g = NG - 1
            gate_stats(g)
            gate_norm(g)
            gate_split(g)
            gate(g)
            weigh_picks(g)
            slots(g)

            def route(ins):
                nonlocal n
                n += 1
                ins.then_inc(dve_const, 1)
                dve.wait_ge(dve_const, n)

            wait(dve, cnt_psum, 1)
            route(dve.tensor_copy(count[:], ps_tok[:, 0:NE]))
            dve.tensor_tensor(tail_row[:], count[:], base_e[:], ALU.add).then_inc(tail_ready, 1)
            dve.memset(ones_e[:], 1.0)
            route(dve.tensor_scalar(cnt_r[:], count[:], float(P - 1), None, ALU.add))
            route(dve.tensor_scalar(cnt_m[:], cnt_r[:], 7, None, ALU.arith_shift_right))
            route(dve.tensor_copy(n_tiles[:], cnt_m[:]))
            route(dve.tensor_tensor_scan(tiles_to[:], ones_e[:], n_tiles[:], 0.0, ALU.mult, ALU.add))
            route(dve.tensor_tensor(past[:], tiles_to[:].unsqueeze(1).broadcast_to([P, 2, NE]), bc(tile_no[:], NE),
                                    ALU.is_le))
            route(dve.tensor_tensor(past_n[:], past[:], n_tiles[:].unsqueeze(1).broadcast_to([P, 2, NE]), ALU.mult))
            dve.tensor_reduce(tile_e[:], past[:], AXX, ALU.add)
            route(dve.tensor_reduce(tile_s[:], past_n[:], AXX, ALU.add))
            route(dve.tensor_tensor(tile_d[:], tile_no[:], tile_s[:], ALU.subtract))
            route(dve.tensor_scalar(tile_d[:], tile_d[:], float(P), None, ALU.mult))
            dve.scalar_tensor_tensor(tile_vals[:, 0:2], tile_e[:], float(REG), tile_d[:], ALU.mult, ALU.add)
            dve.tensor_scalar(tile_vals[:, 2:4], tile_e[:], float(NE - 1), None, ALU.min).then_inc(dve_route, 1)
            wait(dve, table_psum, 1)
            dve.tensor_copy(tile_table[:], ps_pt[0:1, 0:2 * P + HALF]).then_inc(table_ready, 1)

            def hid(i, q):
                wait(dve, *ago(silu_ready, i, q, 0))
                wait(dve, *ago(ht_psum, i, q, 2))
                h2 = (ps_scores, ps_z)[q % 2][:].rearrange("p c (u i h) -> p (c u) i h", u=2, i=2)[:, :, 1, :]
                dve.tensor_tensor(hidden[:, q % 2, :, :], silu[:, q % 2, :, :], h2, ALU.mult).then_inc(hid_ready[q % 2], 1)

            def weigh(i, q):
                wait(dve, *ago(down_psum, i, q, 0))
                wait(dve, rows_out[q], i * 64)
                bank = (ps_tok, ps_pt)[q % 2][:, 0:4 * D].rearrange("p (u f) -> p u f", u=4)
                dve.tensor_tensor(y_rows[:, q, :, :], bank, x_rows[:, q, :, 2 * D:2 * D + 1].broadcast_to([P, 4, D]),
                                  ALU.mult).then_inc(o_ready[q % 2], 1)

            def round_(i, first=False):
                for q in range(QB):
                    if q >= 2:
                        weigh(i, q - 2)
                    elif not first:
                        weigh(i - 1, q - 2 + QB)
                    hid(i, q)

            N = NQ // QB
            round_(0, first=True)
            with dve.Fori(1, N) as i:
                round_(i)
            weigh(N - 1, QB - 2)
            weigh(N - 1, QB - 1)

            for c in range(NCH):
                at = slice(c * CB, (c + 1) * CB)
                wait(dve, x_loaded[c], 64 * N + 32)
                dve.tensor_tensor(resid[:, at, :], resid[:, at, :], picked_out[0][:, at, :], ALU.add).then_inc(added, 1)
                dve.wait_ge(added, c + 1)
                dve.tensor_tensor(resid[:, at, :], resid[:, at, :], picked_out[1][:, at, :], ALU.add)\
                   .then_inc(out_ready, 1)


_INS = ['x', 'mask_BSS_b0_1', 'fside_BSS_rel_dist', 'L0_tok_atom_embed', 'L0_tok_neighbor_embed', 'L0_tok_w_rd',
        'L0_tok_w1', 'L0_tok_b1', 'L0_tok_gamma', 'L0_tok_beta', 'L0_tok_w2', 'L0_tok_b2', 'L0_attn_W_Q',
        'L0_attn_W_K', 'L0_attn_W_V', 'L0_attn_W_O', 'L0_attn_b_Q', 'L0_attn_b_K', 'L0_attn_b_V', 'L0_attn_b_O',
        'L0_ffn_gate_w', 'L0_ffn_gate_b', 'L0_ffn_w1', 'L0_ffn_w2', 'L0_ffn_w3']


def program(nc, arrays):
    args = [nc.dram_tensor(f"in_{name}_dram", a.shape, mybir.dt.from_np(a.dtype), kind="ExternalInput").ap()
            for name, a in arrays.items()]
    NB, S = arrays['x'].shape
    NE, D, _ = arrays['L0_ffn_w1'].shape
    NTOK = NB * S
    out = nc.dram_tensor("out_0_dram", (NB, S, D), F32, kind="ExternalOutput").ap()
    sorted_rows = nc.dram_tensor("sorted_rows", (NE * (NTOK + P) + NE * P, 2 * D + 2), F32).ap()
    expert_out = nc.dram_tensor("expert_out", (2 * NTOK + 2 * NE * P, D), F32).ap()
    lm_tower_kernel(nc, *args, out, sorted_rows, expert_out)


def kernel(**inputs):
    import numpy as _np
    import concourse.bacc as _bacc
    from concourse.bass_utils import run_bass_kernel_spmd as _run

    nc = _bacc.Bacc("TRN2", target_bir_lowering=False, num_devices=1)
    arrays = {}
    for name in _INS:
        a = _np.ascontiguousarray(inputs[name])
        arrays[name] = a
    program(nc, arrays)
    r = _run(nc, [{f"in_{name}_dram": a for name, a in arrays.items()}], core_ids=[0])
    return r.results[0]["out_0_dram"]
```
